# Optimizing a Trainium2 kernel written in Bass

```python
import numpy as np
import jax
import jax.numpy as jnp

def _softmax(x, axis=-1):
    return jax.nn.softmax(x, axis=axis)

def _gelu(x):
    return jax.nn.gelu(x, approximate=True)

def _silu(x):
    return jax.nn.silu(x)

def _sigmoid(x):
    return jax.nn.sigmoid(x)

def _layernorm(x, axis=-1, eps=1e-05):
    m = jnp.mean(x, axis=axis, keepdims=True)
    v = jnp.var(x, axis=axis, keepdims=True)
    return (x - m) / jnp.sqrt(v + eps)

def _scatter_add(tgt, idx, src, axis=0):
    return tgt.at[idx].add(src)

def _segment_sum(src, seg, n):
    return jax.ops.segment_sum(src, seg, n)
kernel_name = 'mk_audio_tower_d1_tok_audfeat512_r4_a30714'

def setup_inputs(seed: int=0):
    np.random.seed(seed)
    _w = jnp.asarray

    def _rec_inputs():
        import jax
        import jax.numpy as jnp
        _rk = jax.random.key(seed)
        x = -7.10856e-05 + 0.999911 * jax.random.normal(jax.random.fold_in(_rk, 1), (64, 375, 128), jnp.float32)
        return x
    x = _rec_inputs()

    def _L0_tok_setup():
        import jax, jax.numpy as jnp
        import numpy as np
        import math
        B, T, D = (32, 1024, 128)
        P, S = (16, 8)
        E = 128

        def _compute_patch_pad(T, P, S):
            if T <= 0:
                return 0
            if T < P:
                return P - T
            n_patches = math.ceil((T - P) / S) + 1
            return max(0, (n_patches - 1) * S + P - T)
        key = jax.random.key(seed)
        k1, k2, k3 = jax.random.split(key, 3)
        x = jax.random.normal(k1, (B, T, D), dtype=jnp.float32)
        bound = 1.0 / math.sqrt(P * D)
        W = jax.random.uniform(k2, (E, P * D), dtype=jnp.float32, minval=-bound, maxval=bound)
        b = jax.random.uniform(k3, (E,), dtype=jnp.float32, minval=-bound, maxval=bound)
        return {'x': x, 'W': W, 'b': b}
    _L0_tok_all = _L0_tok_setup()
    _L0_tok_in = {k: v for k, v in _L0_tok_all.items() if k in ('W', 'b')}
    del _L0_tok_all

    def _L0_attn_setup():
        import jax, jax.numpy as jnp
        import numpy as np
        DIM = 128
        NUM_HEADS = 8
        HEAD_DIM = DIM // NUM_HEADS
        SCALE = HEAD_DIM ** (-0.5)
        key = jax.random.key(seed)
        k_x, k_qkv, k_ow, k_ob = jax.random.split(key, 4)
        B, N = (4, 512)
        x = jax.random.normal(k_x, (B, N, DIM), dtype=jnp.float32)
        w_qkv = jax.random.normal(k_qkv, (DIM, 3 * DIM), dtype=jnp.float32) * DIM ** (-0.5)
        w_out = jax.random.normal(k_ow, (DIM, DIM), dtype=jnp.float32) * DIM ** (-0.5)
        b_out = jax.random.normal(k_ob, (DIM,), dtype=jnp.float32) * 0.01
        return {'x': x, 'w_qkv': w_qkv, 'w_out': w_out, 'b_out': b_out}
    _L0_attn_all = _L0_attn_setup()
    _L0_attn_in = {k: v for k, v in _L0_attn_all.items() if k in ('w_qkv', 'w_out', 'b_out')}
    del _L0_attn_all

    def _L0_ffn_setup():
        import jax, jax.numpy as jnp
        import numpy as np
        B, T, DIM = (2, 64, 128)
        E, H, K = (64, 256, 42)
        key = jax.random.key(seed)
        ks = jax.random.split(key, 7)
        s1 = 1.0 / np.sqrt(DIM).astype(np.float32)
        s2 = 1.0 / np.sqrt(H).astype(np.float32)
        return {'x': jax.random.normal(ks[0], (B, T, DIM), jnp.float32), 'w1': jax.random.uniform(ks[1], (E, DIM, H), jnp.float32, -s1, s1), 'b1': jax.random.uniform(ks[2], (E, H), jnp.float32, -s1, s1), 'w2': jax.random.uniform(ks[3], (E, H, DIM), jnp.float32, -s2, s2), 'b2': jax.random.uniform(ks[4], (E, DIM), jnp.float32, -s2, s2), 'router_w': jax.random.uniform(ks[5], (DIM, E), jnp.float32, -s1, s1), 'router_b': jax.random.uniform(ks[6], (E,), jnp.float32, -s1, s1)}
    _L0_ffn_all = _L0_ffn_setup()
    _L0_ffn_in = {k: v for k, v in _L0_ffn_all.items() if k in ('w1', 'b1', 'w2', 'b2', 'router_w', 'router_b')}
    del _L0_ffn_all
    return {'x': x, 'L0_tok_W': _L0_tok_in['W'], 'L0_tok_b': _L0_tok_in['b'], 'L0_attn_w_qkv': _L0_attn_in['w_qkv'], 'L0_attn_w_out': _L0_attn_in['w_out'], 'L0_attn_b_out': _L0_attn_in['b_out'], 'L0_ffn_w1': _L0_ffn_in['w1'], 'L0_ffn_b1': _L0_ffn_in['b1'], 'L0_ffn_w2': _L0_ffn_in['w2'], 'L0_ffn_b2': _L0_ffn_in['b2'], 'L0_ffn_router_w': _L0_ffn_in['router_w'], 'L0_ffn_router_b': _L0_ffn_in['router_b']}

def reference(x, L0_tok_W, L0_tok_b, L0_attn_w_qkv, L0_attn_w_out, L0_attn_b_out, L0_ffn_w1, L0_ffn_b1, L0_ffn_w2, L0_ffn_b2, L0_ffn_router_w, L0_ffn_router_b):
    import jax
    import jax.numpy as jnp

    def _L0_tok_ref(x, W, b):
        import jax, jax.numpy as jnp
        import numpy as np
        import math
        B, T, D = (32, 1024, 128)
        P, S = (16, 8)
        E = 128

        def _compute_patch_pad(T, P, S):
            if T <= 0:
                return 0
            if T < P:
                return P - T
            n_patches = math.ceil((T - P) / S) + 1
            return max(0, (n_patches - 1) * S + P - T)
        Bx, Tx, Dx = x.shape
        pad = _compute_patch_pad(Tx, P, S)
        if pad > 0:
            x = jnp.pad(x, ((0, 0), (0, pad), (0, 0)))
        T_pad = x.shape[1]
        Np = (T_pad - P) // S + 1
        idx = jnp.arange(Np)[:, None] * S + jnp.arange(P)[None, :]
        patches = x[:, idx, :]
        Wr = W.reshape(E, Dx, P)
        tokens = jnp.einsum('bnpd,edp->bne', patches, Wr) + b
        return tokens

    def _L0_attn_ref(x, w_qkv, w_out, b_out):
        import jax, jax.numpy as jnp
        import numpy as np
        DIM = 128
        NUM_HEADS = 8
        HEAD_DIM = DIM // NUM_HEADS
        SCALE = HEAD_DIM ** (-0.5)
        B, N, C = x.shape
        qkv = jnp.einsum('bnc,cd->bnd', x, w_qkv)
        qkv = qkv.reshape(B, N, 3, NUM_HEADS, HEAD_DIM)
        qkv = jnp.transpose(qkv, (2, 0, 3, 1, 4))
        q, k, v = (qkv[0], qkv[1], qkv[2])
        attn = jnp.einsum('bhqd,bhkd->bhqk', q, k) * SCALE
        attn = jax.nn.softmax(attn, axis=-1)
        o = jnp.einsum('bhqk,bhkd->bhqd', attn, v)
        o = jnp.transpose(o, (0, 2, 1, 3)).reshape(B, N, C)
        return jnp.einsum('bnc,cd->bnd', o, w_out) + b_out

    def _L0_ffn_ref(x, w1, b1, w2, b2, router_w, router_b):
        import jax, jax.numpy as jnp
        import numpy as np
        B, T, DIM = (2, 64, 128)
        E, H, K = (64, 256, 42)
        Bb, Tt, C = x.shape
        N = Bb * Tt
        logits = x @ router_w + router_b
        probs = jax.nn.softmax(logits, axis=-1)
        top_w, top_idx = jax.lax.top_k(probs, K)
        top_w = jax.nn.softmax(top_w, axis=-1)
        xt = x.reshape(N, C)
        top_w = top_w.reshape(N, K)
        top_idx = top_idx.reshape(N, K)
        comb = jnp.zeros((N, E), x.dtype).at[jnp.arange(N)[:, None], top_idx].set(top_w)
        h = jax.nn.gelu(jnp.einsum('td,edh->teh', xt, w1) + b1, approximate=False)
        y = jnp.einsum('teh,ehd->ted', h, w2) + b2
        out = jnp.einsum('ted,te->td', y, comb)
        return out.reshape(Bb, Tt, C)
    h = _L0_tok_ref(x, L0_tok_W, L0_tok_b)
    h = h + _L0_attn_ref(_layernorm(h, axis=-1), L0_attn_w_qkv, L0_attn_w_out, L0_attn_b_out)
    h = h + _L0_ffn_ref(_layernorm(h, axis=-1), L0_ffn_w1, L0_ffn_b1, L0_ffn_w2, L0_ffn_b2, L0_ffn_router_w, L0_ffn_router_b)
    return h

_drawn_inputs = setup_inputs


def setup_inputs(seed=0):
    import zlib

    import numpy as np

    out = dict(_drawn_inputs(seed))
    spreads = {}
    factors = {'L0_attn_b_out': 3.366, 'L0_ffn_b1': 8.0, 'L0_ffn_b2': 6.39, 'L0_ffn_router_b': 6.047}
    for name, (base, spread) in spreads.items():
        noise = np.random.default_rng([zlib.crc32(name.encode()), seed]).standard_normal(out[name].shape)
        drawn = base * np.exp(spread * noise) if base else spread * noise
        out[name] = jnp.asarray(drawn.astype(out[name].dtype))
    for name, factor in factors.items():
        out[name] = (out[name] * factor).astype(out[name].dtype)
    return out
```

```python
from contextlib import ExitStack

import concourse.bass as bass
from concourse import mybir

ALU = mybir.AluOpType
ACT = mybir.ActivationFunctionType
F32 = mybir.dt.float32
F32R = mybir.dt.float32r
AX_X = mybir.AxisListType.X

P = 128
EPS = 1e-5
PATCH, STRIDE = 16, 8
HEADS = 8
TOPK = 42
TAKEN = -2.0


def audio_tower(nc, x, tok_W, tok_b, w_qkv, w_out, b_out, w1, b1, w2, b2, router_w, router_b, out):
    B, T, D = x.shape
    E, _, H = w1.shape
    N = out.shape[1]
    M = N + 1
    HD = D // HEADS
    SCALE = float(HD) ** -0.5
    PAIRS = B // 2
    PN, PM = 2 * N, 2 * M
    TOK = B * N
    GP = 4
    GROUPS = PAIRS // GP
    GN = GP * PN
    TILES = TOK // P
    assert D == P and TOK % P == 0 and H == 2 * P and E * 2 == P and PATCH == 2 * STRIDE

    BLK = 512
    blocks = [(s, min(BLK, TOK - s)) for s in range(0, TOK, BLK)]
    NB = len(blocks)
    NG = NB // 2
    chunks = [(blocks[2 * c][0], blocks[2 * c][1] + blocks[2 * c + 1][1]) for c in range(NG)]
    HALVES = 2 * E
    DROP = E - TOPK
    ROUNDS = -(-DROP // 8)
    LASTDROP = DROP - 8 * (ROUNDS - 1)

    comb_dram = nc.dram_tensor("comb_scratch", (E, TOK), F32).ap()

    with ExitStack() as ctx:
        def sb(name, shape, dt=F32):
            return ctx.enter_context(nc.sbuf_tensor(name, shape, dt))

        def sem(name):
            return ctx.enter_context(nc.semaphore(name))

        ps = ctx.enter_context(nc.psum_tensor("ps", [P, 8, BLK], F32))

        ident = sb("ident", [P, P])
        ones_mean = sb("ones_mean", [P, P])
        ones_row = sb("ones_row", [1, P])
        eps_col = sb("eps_col", [P, 1])
        head_mask = sb("head_mask", [P, HEADS])
        parity_mask = sb("parity_mask", [PN, 2, HD])
        W_raw = sb("W_raw", [P, D * PATCH])
        WT = sb("WT", [P, PATCH, P])
        bias_cols = sb("bias_cols", [P, 2])
        wqkv_sb = sb("wqkv_sb", [P, 3 * D])
        wout_sb = sb("wout_sb", [P, D])
        rw_sb = sb("rw_sb", [P, E])
        rb_sb = sb("rb_sb", [1, E])
        b1_raw = sb("b1_raw", [P, P])
        b1T = sb("b1T", [P, HALVES])
        b2_sb = sb("b2_sb", [E, D])
        b1_col = sb("b1_col", [P, 4, 1])
        zeros2 = sb("zeros2", [P, 4])
        pool_tick = sb("pool_tick", [P, 1])

        hT = sb("hT", [P, TOK])

        gbuf = sb("gbuf", [P, 2, TOK])
        cbuf = sb("cbuf", [P, 2, TOK])
        g_hi = sb("g_hi", [P, 2, TOK], F32R)
        g_lo = sb("g_lo", [P, 2, TOK], F32R)
        x_hi = sb("x_hi", [P, TOK], F32R)
        x_lo = sb("x_lo", [P, TOK], F32R)
        w_raw = sb("w_raw", [P, 2, 2 * H])
        w_hi = sb("w_hi", [P, 2, 2 * H], F32R)
        w_lo = sb("w_lo", [P, 2, 2 * H], F32R)

        gflat = gbuf[:, :, :].rearrange("p a b -> p (a b)")
        cflat = cbuf[:, :, :].rearrange("p a b -> p (a b)")
        xin = gflat[:, 0:GP * STRIDE * D].rearrange("p (a b) -> p a b", a=GP)
        xT = cflat[:, 0:STRIDE * GP * PM].rearrange("p (r a m) -> p r a m", r=STRIDE, a=GP)
        LN0 = STRIDE * GP * PM
        xc = cflat[:, LN0:LN0 + 2 * GN].rearrange("p (s n) -> p s n", s=2)
        sq = cflat[:, LN0 + 2 * GN:LN0 + 4 * GN].rearrange("p (s n) -> p s n", s=2)
        xn = gflat[:, TOK:2 * TOK]
        at = [0]

        def carve(cols):
            at[0] += cols
            return cflat[:, at[0] - cols:at[0]]

        q_st = carve(2 * 128).rearrange("p (s b n) -> p s b n", s=2, b=2)
        x_st = carve(2 * 4 * N).rearrange("p (s b c n) -> p s b c n", s=2, b=2, c=2)
        k_blk = carve(4 * HEADS * N).rearrange("p (s b h n) -> p s b h n", s=2, b=2, h=HEADS)
        v_blk = carve(4 * D).rearrange("p (s b d) -> p s b d", s=2, b=2)
        prob = carve(2 * HEADS * N).rearrange("p (s h n) -> p s h n", s=2, h=HEADS)
        pT = carve(8 * P).rearrange("p (s c n) -> p s c n", s=2, c=4)
        o_st = gflat[:, 0:2 * PN].rearrange("p (s n) -> p s n", s=2)
        smax = gflat[:, 256:256 + 2 * HEADS].rearrange("p (s h) -> p s h", s=2)
        ssum = gflat[:, 288:288 + 2 * HEADS].rearrange("p (s h) -> p s h", s=2)
        assert at[0] <= 2 * TOK
        RW = TILES * E
        rp = cflat[:, 0:RW].rearrange("p (t e) -> p t e", e=E)
        re = cflat[:, RW:2 * RW].rearrange("p (t e) -> p t e", e=E)
        rs = cflat[:, 2 * RW:3 * RW].rearrange("p (t e) -> p t e", e=E)
        rtop = gflat[:, 0:8 * TILES].rearrange("p (t k) -> p t k", k=8)
        rmax = gflat[:, 256:256 + TILES]
        rsum = gflat[:, 288:288 + TILES]
        pmax = gflat[:, 320:320 + TILES]
        combT = gflat[0:E, 384:384 + TOK]
        yT = gflat[:, 0:TOK]
        y_st = cflat[:, 0:PAIRS * D].rearrange("p (a d) -> p a d", d=D)
        assert PAIRS * D <= 2 * TOK

        s_const = sem("s_const")
        s_bias = sem("s_bias")
        s_small = sem("s_small")
        s_wraw = sem("s_wraw")
        s_wt = sem("s_wt")
        s_wt_out = sem("s_wt_out")
        s_xzero = sem("s_xzero")
        s_xin = [sem(f"s_xin{p}") for p in range(GP)]
        s_xt = sem("s_xt")
        s_xt_out = sem("s_xt_out")
        s_tok = sem("s_tok")
        s_tok_out = sem("s_tok_out")
        ln = [{k: sem(f"s_ln{a}_{k}") for k in ("mean", "xc", "sq", "var", "sd", "rs", "xn")} for a in range(2)]
        at_s = {k: sem(f"s_at_{k}") for k in ("xst", "qk", "q", "k", "v", "vm", "s", "mx", "sub", "exp", "sum", "rec", "p",
                                              "t", "pt", "o", "ost", "pr", "res", "zero")}
        r_s = {k: sem(f"s_r_{k}") for k in ("xh", "lg", "dve", "act", "t", "ct", "dram")}
        s_b1t = sem("s_b1t")
        s_b1 = sem("s_b1")
        w_loaded = [sem(f"w_loaded{s}") for s in range(2)]
        c_loaded = [sem(f"c_loaded{s}") for s in range(2)]
        w_split = sem("w_split")
        s_tick = sem("s_tick")
        b1_ready = sem("b1_ready")
        w_hi_done = sem("w_hi_done")
        up_done = sem("up_done")
        gelu_done = sem("gelu_done")
        mul_done = sem("mul_done")
        hi_done = sem("hi_done")
        lo_done = sem("lo_done")
        down_done = sem("down_done")
        s_acc = sem("s_acc")
        s_y = sem("s_y")
        s_yt = sem("s_yt")
        s_yst = sem("s_yst")
        s_out = sem("s_out")

        block = ctx.enter_context(nc.Block())

        XT_STEPS = 2 * GP
        EX2 = E // 2 - 1

        @block.sync
        def _(sp):
            nc_ = sp
            nc_.dma_start(W_raw[:, :], tok_W).then_inc(s_wraw, 16)
            sp.wait_ge(s_xzero, 1)

            def frames(g, p):
                pair = g * GP + p
                rows = x[bass.ds(2 * pair, 2), 0:N * STRIDE, :].rearrange("b (m r) d -> m b (r d)", r=STRIDE)
                sp.dma_start(xin[0:PN, p, :], rows).then_inc(s_xin[p], 16)
                rest = x[bass.ds(2 * pair, 2), N * STRIDE:T, :].rearrange("b r d -> b (r d)")
                sp.dma_start(xin[PN:PM, p, 0:(T - N * STRIDE) * D], rest).then_inc(s_xin[p], 16)

            for p in range(GP):
                frames(0, p)
            small = [(bias_cols[:, 0:1], tok_b.rearrange("(p a) -> p a", a=1)),
                     (bias_cols[:, 1:2], b_out.rearrange("(p a) -> p a", a=1)),
                     (wqkv_sb[:, :], w_qkv), (wout_sb[:, :], w_out), (rw_sb[:, :], router_w),
                     (rb_sb[:, :], router_b.rearrange("(a e) -> a e", a=1)),
                     (b1_raw[:, :], b1.rearrange("e (j h) -> (e j) h", j=2)), (b2_sb[:, :], b2)]
            for dst, src in small:
                sp.dma_start(dst, src).then_inc(s_small, 16)
            with sp.Fori(1, GROUPS) as g:
                for p in range(GP):
                    sp.wait_ge(s_xt, (g - 1) * XT_STEPS + 2 * p + 2)
                    frames(g, p)

            def weights(e, slot):
                sp.dma_start(w_raw[:, slot, 0:H], w1[bass.ds(e, 1), :, :].rearrange("a d h -> d (a h)")).then_inc(w_loaded[slot], 16)
                sp.dma_start(w_raw[:, slot, H:2 * H].rearrange("p (j d) -> p j d", j=2),
                             w2[bass.ds(e, 1), :, :].rearrange("a (j p) d -> p (a j) d", j=2)).then_inc(w_loaded[slot], 16)

            def combine(e, slot):
                sp.dma_start(cbuf[:, slot, :], comb_dram[bass.ds(e, 1), :].to_broadcast([P, TOK])).then_inc(c_loaded[slot], 16)

            for e in range(2):
                weights(e, e)
            sp.wait_ge(r_s["t"], TILES)
            sp.wait_ge(r_s["ct"], NB)
            sp.dma_start(comb_dram, combT).then_inc(r_s["dram"], 16)
            sp.wait_ge(r_s["dram"], 16)
            for e in range(2):
                combine(e, e)
            with sp.Fori(0, EX2) as i:
                for slot in range(2):
                    sp.wait_ge(w_split, 2 * i + slot + 1)
                    weights(2 * i + 2 + slot, slot)
                    sp.wait_ge(mul_done, (2 * i + slot + 1) * 2 * NG)
                    combine(2 * i + 2 + slot, slot)

            for p in range(PAIRS):
                if p % 4 == 0:
                    sp.wait_ge(s_yst, p // 4 + 1)
                sp.dma_start(out[2 * p:2 * p + 2, :, :].rearrange("b n d -> n b d"), y_st[0:PN, p, :]).then_inc(s_out, 16)
            sp.wait_ge(s_out, 16 * PAIRS)

        @block.gpsimd
        def _(pool):
            pool.memset(gflat[:, 0:GP * STRIDE * D], 0.0).then_inc(s_xzero, 1)
            pool.memset(pool_tick[:, :], 0.0).then_inc(s_tick, 1)
            pool.memset(ident[:, :], 0.0).then_inc(s_const, 1)
            pool.memset(ones_mean[:, :], 1.0 / D).then_inc(s_const, 1)
            pool.memset(ones_row[:, :], 1.0).then_inc(s_const, 1)
            pool.memset(eps_col[:, :], EPS).then_inc(s_const, 1)
            pool.memset(head_mask[:, :], 1.0).then_inc(s_const, 1)
            pool.memset(parity_mask[:, :, :], 1.0).then_inc(s_const, 1)
            pool.memset(zeros2[:, :], 0.0).then_inc(s_const, 1)
            pool.wait_ge(s_const, 7)
            pool.affine_select(out=ident[:, :], in_=ident[:, :], compare_op=ALU.not_equal, fill=1.0, base=0,
                               pattern=[[-1, P]], channel_multiplier=1).then_inc(s_const, 1)
            pool.affine_select(out=head_mask[:, :], in_=head_mask[:, :], compare_op=ALU.is_ge, fill=0.0, base=0,
                               pattern=[[-HD, HEADS]], channel_multiplier=1).then_inc(s_const, 1)
            pool.affine_select(out=parity_mask[:, 0, :], in_=parity_mask[:, 0, :], compare_op=ALU.is_ge, fill=0.0,
                               base=N - 1, pattern=[[0, HD]], channel_multiplier=-1).then_inc(s_const, 1)
            pool.affine_select(out=parity_mask[:, 1, :], in_=parity_mask[:, 1, :], compare_op=ALU.is_ge, fill=0.0,
                               base=-N, pattern=[[0, HD]], channel_multiplier=1).then_inc(s_const, 1)
            pool.wait_ge(s_const, 11)
            pool.affine_select(out=head_mask[:, :], in_=head_mask[:, :], compare_op=ALU.is_ge, fill=0.0, base=HD - 1,
                               pattern=[[HD, HEADS]], channel_multiplier=-1).then_inc(s_const, 1)
            pool.wait_ge(ln[0]["xn"], GROUPS)
            pool.memset(q_st[:, :, :, :], 0.0).then_inc(at_s["zero"], 1)

            def stage(i, s):
                if s is not None:
                    src = xn[:, bass.ds(i * PN, PN)].rearrange("p (n b) -> p b n", b=2)
                    for c in range(2):
                        pool.tensor_copy(x_st[:, s, :, c, :], src).then_inc(at_s["xst"], 1)

            for s in range(2):
                stage(s, s)
            with pool.Fori(0, PAIRS // 2 - 1) as j:
                for s in range(2):
                    pool.wait_ge(at_s["v"], 2 * j + s + 1)
                    stage(2 * j + 2 + s, s)

            def split(e, slot, use):
                first = isinstance(use, int)
                pool.wait_ge(w_loaded[slot], 32 * (use + 1))
                if not first:
                    pool.wait_ge(s_tick, e - 1)
                    pool.wait_ge(down_done, (e - 1) * 2 * NG)
                    pool.tensor_tensor(pool_tick[:, :], eps_col[:, :], eps_col[:, :], ALU.add).then_inc(s_tick, 1)
                pool.tensor_copy(w_hi[:, slot, :], w_raw[:, slot, :]).then_inc(w_hi_done, 1)
                pool.wait_ge(w_hi_done, e + 1)
                pool.tensor_tensor(w_lo[:, slot, :], w_raw[:, slot, :], w_hi[:, slot, :].bitcast(F32),
                                   ALU.subtract).then_inc(w_split, 1)

            for e in range(2):
                split(e, e, 0)
            with pool.Fori(0, EX2) as i:
                for slot in range(2):
                    split(2 * i + 2 + slot, slot, i + 1)

        @block.tensor
        def _(pe):
            pe.wait_ge(s_const, 12)
            pe.wait_ge(s_wraw, 16)
            Wv = W_raw[:, :].rearrange("e (d f) -> e f d", f=PATCH)
            for f in range(PATCH):
                if f >= 8 and f % 4 == 0:
                    pe.wait_ge(s_wt_out, f // 4 - 1)
                mm = pe.transpose(ps[:, f // 4 % 2, f % 4 * P:(f % 4 + 1) * P], Wv[:, f, :], ident[:, :])
                if f % 4 == 3:
                    mm.then_inc(s_wt, 1)
            pe.wait_ge(s_wt_out, 4)

            def transpose_frames(g, first):
                for p in range(GP):
                    pe.wait_ge(s_xin[p], 32 * (g + 1))
                    for half in range(2):
                        step = 2 * p + half
                        bank = step % 4
                        if not (first and step < 4):
                            pe.wait_ge(s_xt_out, g * XT_STEPS + step - 3)
                        for k in range(4):
                            r = 4 * half + k
                            mm = pe.transpose(ps[:, bank, k * PM:(k + 1) * PM], xin[0:PM, p, r * D:(r + 1) * D],
                                              ident[0:PM, 0:PM])
                        mm.then_inc(s_xt, 1)

            def embed(g, first):
                pe.wait_ge(s_xt_out, (g + 1) * XT_STEPS)
                if not first:
                    pe.wait_ge(s_tok_out, g)
                for f in range(PATCH):
                    r, s = f % STRIDE, f // STRIDE
                    mm = pe.matmul(ps[:, 4, 0:GN], WT[:, f, :], xT[:, r, :, 2 * s:2 * s + PN],
                                   start=(f == 0), stop=(f == PATCH - 1))
                mm.then_inc(s_tok, 1)

            transpose_frames(0, True)
            embed(0, True)
            with pe.Fori(1, GROUPS) as g:
                transpose_frames(g, False)
                embed(g, False)

            def layer_norm(a):
                pe.wait_ge(s_tok_out if a == 0 else at_s["res"], GROUPS if a == 0 else PAIRS)

                def mean(g, slot, free):
                    if free is not None:
                        pe.wait_ge(ln[a]["xc"], free)
                    pe.matmul(ps[:, slot, 0:GN], ones_mean[:, :], hT[:, bass.ds(g * GN, GN)],
                              start=True, stop=True).then_inc(ln[a]["mean"], 1)

                def var(g, slot, free):
                    pe.wait_ge(ln[a]["sq"], g + 1)
                    if free is not None:
                        pe.wait_ge(ln[a]["sd"], free)
                    pe.matmul(ps[:, 2 + slot, 0:GN], ones_mean[:, :], sq[:, slot, :],
                              start=True, stop=True).then_inc(ln[a]["var"], 1)

                mean(0, 0, None)
                mean(1, 1, None)
                var(0, 0, None)
                mean(2, 0, 1)
                var(1, 1, None)
                mean(3, 1, 2)
                with pe.Fori(1, GROUPS // 2 - 1) as j:
                    for s in range(2):
                        var(2 * j + s, s, 2 * j + s - 1)
                        mean(2 * j + 2 + s, s, 2 * j + 1 + s)
                for g in (GROUPS - 2, GROUPS - 1):
                    var(g, g % 2, g - 1)

            layer_norm(0)

            pe.wait_ge(s_small, 16 * 8)
            pe.wait_ge(ln[0]["xn"], GROUPS)

            def scores(i, s, first):
                tok = xn[:, bass.ds(i * PN, PN)]
                if not first:
                    pe.wait_ge(at_s["q"], i - 1)
                    pe.wait_ge(at_s["k"], i - 1)
                pe.matmul(ps[:, s, 0:PN], wqkv_sb[:, 0:D], tok, start=True, stop=True)
                pe.matmul(ps[:, s, PN:2 * PN], wqkv_sb[:, D:2 * D], tok, start=True, stop=True).then_inc(at_s["qk"], 1)
                pe.wait_ge(at_s["xst"], 2 * i + 2)
                if not first:
                    pe.wait_ge(at_s["vm"], i - 1)
                for b in range(2):
                    mm = pe.matmul(ps[0:PN, 2 + s, b * D:(b + 1) * D], x_st[:, s, b, :, :], wqkv_sb[:, 2 * D:3 * D],
                                   start=True, stop=True)
                mm.then_inc(at_s["v"], 1)
                pe.wait_ge(at_s["q"], i + 1)
                pe.wait_ge(at_s["k"], i + 1)
                if not first:
                    pe.wait_ge(at_s["sub"], i - 1)
                for b in range(2):
                    mm = pe.matmul(ps[64 * b:64 * b + 64, 4 + s, 0:HEADS * N], q_st[:, s, b, :], k_blk[:, s, b, :, :],
                                   start=True, stop=True)
                mm.then_inc(at_s["s"], 1)

            def weigh(i, s, first):
                pe.wait_ge(at_s["p"], i + 1)
                if not first:
                    pe.wait_ge(at_s["pt"], i)
                for c in range(4):
                    mm = pe.transpose(ps[0:PN, 6, c * P:(c + 1) * P], prob[:, s, 2 * c:2 * c + 2, :], ident[:, :])
                mm.then_inc(at_s["t"], 1)
                pe.wait_ge(at_s["pt"], i + 1)
                pe.wait_ge(at_s["vm"], i + 1)
                if not first:
                    pe.wait_ge(at_s["res"], i)
                for c in range(4):
                    for b in range(2):
                        mm = pe.matmul(ps[32 * c:32 * c + 32, 7, b * N:(b + 1) * N], v_blk[0:PN, s, b, 32 * c:32 * c + 32],
                                       pT[0:PN, s, c, 64 * b:64 * b + N], start=True, stop=True)
                mm.then_inc(at_s["o"], 1)
                pe.wait_ge(at_s["ost"], i + 1)
                pe.matmul(ps[:, 7, 256:256 + PN], wout_sb[:, :], o_st[:, s, :], start=True, stop=True).then_inc(at_s["pr"], 1)

            scores(0, 0, True)
            scores(1, 1, True)
            weigh(0, 0, True)
            with pe.Fori(1, PAIRS // 2) as j:
                scores(2 * j, 0, False)
                weigh(2 * j - 1, 1, False)
                scores(2 * j + 1, 1, False)
                weigh(2 * j, 0, False)
            weigh(PAIRS - 1, 1, False)

            layer_norm(1)

            pe.wait_ge(ln[1]["xn"], GROUPS)
            for t in range(TILES):
                o = ps[:, t // 8, t % 8 * E:(t % 8 + 1) * E]
                pe.matmul(o, xn[:, t * P:(t + 1) * P], rw_sb[:, :], start=True, stop=False)
                mm = pe.matmul(o, ones_row[:, :], rb_sb[:, :], start=False, stop=True)
            mm.then_inc(r_s["lg"], 1)
            pe.transpose(ps[:, 3, 0:P], b1_raw[:, :], ident[:, :]).then_inc(s_b1t, 1)
            pe.wait_ge(r_s["dve"], RDVE)
            for t in range(TILES):
                bank = 4 + t // 4 % 2
                if t >= 8 and t % 4 == 0:
                    pe.wait_ge(r_s["ct"], t // 4 - 1)
                pe.transpose(ps[0:E, bank, t % 4 * P:(t % 4 + 1) * P], re[:, t, :], ident[:, :]).then_inc(r_s["t"], 1)
            pe.wait_ge(r_s["ct"], NB)
            for t, (s, n) in enumerate(blocks):
                pe.matmul(ps[:, t, 0:n], b2_sb[:, :], combT[:, s:s + n], start=True, stop=False, skip_group_check=True)
            pe.wait_ge(s_b1, 1)
            pe.wait_ge(r_s["xh"], 2)

            def up(k0, t, w, free):
                s, n = blocks[t]
                slot, j = w
                if free:
                    pe.wait_ge(gelu_done, k0 + t - 1)
                cols = slice(j * P, (j + 1) * P)
                o = ps[:, 6 + t % 2, 0:n]
                pe.matmul(o, w_hi[:, slot, cols], x_lo[:, s:s + n], start=True, stop=False)
                pe.matmul(o, w_lo[:, slot, cols], x_hi[:, s:s + n], start=False, stop=False)
                pe.matmul(o, w_hi[:, slot, cols], x_hi[:, s:s + n], start=False, stop=True).then_inc(up_done, 1)

            def down(m0, t, w, gs):
                s, n = blocks[t]
                slot, j = w
                if t % 2 == 0:
                    pe.wait_ge(lo_done, m0 + t // 2 + 1)
                cols = slice(H + j * P, H + (j + 1) * P)
                o = ps[:, t, 0:n]
                pe.matmul(o, w_hi[:, slot, cols], g_lo[:, gs, s:s + n], start=False, stop=False, skip_group_check=True)
                pe.matmul(o, w_lo[:, slot, cols], g_hi[:, gs, s:s + n], start=False, stop=False, skip_group_check=True)
                mm = pe.matmul(o, w_hi[:, slot, cols], g_hi[:, gs, s:s + n], start=False, stop=False, skip_group_check=True)
                if t % 2 == 1:
                    mm.then_inc(down_done, 1)

            def step(n, q):
                for t in range(NB):
                    if t == 0 and q % 2 == 0:
                        pe.wait_ge(w_split, (n + 2) // 2 if isinstance(n, int) else n[1])
                    nn = n if isinstance(n, int) else n[0]
                    up(nn * NB, t, (q // 2, q % 2), True)
                    pq = (q - 1) % 4
                    down((nn - 1) * NG, t, (pq // 2, pq % 2), pq % 2)

            pe.wait_ge(w_split, 1)
            for t in range(NB):
                up(0, t, (0, 0), t >= 2)
            with pe.Fori(0, EX2) as i:
                for q in range(4):
                    step((4 * i + 1 + q, 2 * i + (q + 3) // 2), (1 + q) % 4)
            for n in range(4 * EX2 + 1, HALVES):
                step(n, n % 4)
            for t in range(NB):
                down((HALVES - 1) * NG, t, (1, 1), 1)
            for t, (s, n) in enumerate(blocks):
                pe.matmul(ps[:, t, 0:n], ident[:, :], hT[:, s:s + n], start=False, stop=True,
                          skip_group_check=True).then_inc(s_acc, 1)
            for p in range(PAIRS):
                if p % 4 == 0:
                    pe.wait_ge(s_y, NB if p == 0 else NB)
                    if p >= 8:
                        pe.wait_ge(s_yst, p // 4 - 1)
                mm = pe.transpose(ps[0:PN, 6 + p // 4 % 2, p % 4 * D:(p % 4 + 1) * D], yT[:, p * PN:(p + 1) * PN], ident[:, :])
                if p % 4 == 3:
                    mm.then_inc(s_yt, 1)

        @block.scalar
        def _(act):
            for c in range(4):
                act.wait_ge(s_wt, c + 1)
                act.activation(WT[:, 4 * c:4 * c + 4, :], ps[:, c % 2, :].rearrange("p (f e) -> p f e", f=4),
                               ACT.Copy).then_inc(s_wt_out, 1)

            act.wait_ge(s_small, 16 * 8)

            def frames_out(g, first):
                for p in range(GP):
                    act.wait_ge(s_xt, g * XT_STEPS + 2 * p + 1)
                    if p == 0 and not first:
                        act.wait_ge(s_tok, g)
                    if p or not first:
                        act.wait_ge(s_xt_out, g * XT_STEPS + 2 * p)
                    act.activation(xT[:, 0:4, p, :], ps[:, 2 * p % 4, 0:4 * PM].rearrange("p (r m) -> p r m", r=4),
                                   ACT.Copy).then_inc(s_xt_out, 1)
                act.wait_ge(s_tok, g + 1)
                act.activation(hT[:, bass.ds(g * GN, GN)], ps[:, 4, 0:GN], ACT.Identity,
                               bias=bias_cols[:, 0:1]).then_inc(s_tok_out, 1)

            frames_out(0, True)
            with act.Fori(1, GROUPS) as g:
                frames_out(g, False)

            def layer_norm(a):
                def square(g, slot, free):
                    act.wait_ge(ln[a]["xc"], g + 1)
                    if free is not None:
                        act.wait_ge(ln[a]["var"], free)
                    act.activation(sq[:, slot, :], xc[:, slot, :], ACT.Square).then_inc(ln[a]["sq"], 1)

                def root(g, slot):
                    act.wait_ge(ln[a]["var"], g + 1)
                    act.activation(sq[:, slot, :], ps[:, 2 + slot, 0:GN], ACT.Sqrt, bias=eps_col[:, :]).then_inc(ln[a]["sd"], 1)

                square(0, 0, None)
                square(1, 1, None)
                with act.Fori(0, GROUPS // 2 - 1) as j:
                    for s in range(2):
                        root(2 * j + s, s)
                        act.wait_ge(ln[a]["xn"], 2 * j + s + 1)
                        square(2 * j + 2 + s, s, None)
                for s in range(2):
                    root(GROUPS - 2 + s, s)

            layer_norm(0)

            act.wait_ge(at_s["zero"], 1)

            def head(i, s):
                act.wait_ge(at_s["qk"], i + 1)
                act.activation(q_st[:, s, :, 0:N], ps[:, s, 0:PN].rearrange("p (n b) -> p b n", b=2),
                               ACT.Copy, scale=SCALE).then_inc(at_s["q"], 1)

            def tail(i, s):
                act.wait_ge(at_s["sub"], i + 1)
                act.activation(prob[:, s, :, :], prob[:, s, :, :], ACT.Exp).then_inc(at_s["exp"], 1)

            def late(i, s):
                act.wait_ge(at_s["t"], i + 1)
                act.activation(pT[0:PN, s, :, :], ps[0:PN, 6, :].rearrange("p (c n) -> p c n", c=4),
                               ACT.Copy).then_inc(at_s["pt"], 1)
                act.wait_ge(at_s["o"], i + 1)
                act.activation(o_st[:, s, :].rearrange("p (n b) -> p b n", b=2),
                               ps[:, 7, 0:PN].rearrange("p (b n) -> p b n", b=2), ACT.Copy).then_inc(at_s["ost"], 1)

            head(0, 0)
            tail(0, 0)
            head(1, 1)
            tail(1, 1)
            late(0, 0)
            with act.Fori(1, PAIRS // 2) as j:
                head(2 * j, 0)
                tail(2 * j, 0)
                late(2 * j - 1, 1)
                head(2 * j + 1, 1)
                tail(2 * j + 1, 1)
                late(2 * j, 0)
            late(PAIRS - 1, 1)

            layer_norm(1)

            act.wait_ge(ln[1]["xn"], GROUPS)
            act.activation(x_hi[:, :], xn, ACT.Copy).then_inc(r_s["xh"], 1)
            act.wait_ge(r_s["dve"], 2)
            act.activation(rp[:, :, :], rp[:, :, :], ACT.Exp).then_inc(r_s["act"], 1)
            act.wait_ge(s_b1t, 1)
            act.activation(b1T[:, :], ps[:, 3, 0:P], ACT.Copy).then_inc(s_b1, 1)
            act.wait_ge(r_s["dve"], 7)
            act.activation(re[:, :, :], re[:, :, :], ACT.Exp).then_inc(r_s["act"], 1)
            for t, (s, n) in enumerate(blocks):
                act.wait_ge(r_s["t"], min(4 * t + 4, TILES))
                act.activation(combT[:, s:s + n], ps[0:E, 4 + t % 2, 0:n], ACT.Copy).then_inc(r_s["ct"], 1)
            act.wait_ge(r_s["dram"], 16)
            act.wait_ge(up_done, 1)

            def gelu(n, t, gs, b):
                s, m = blocks[t]
                act.wait_ge(up_done, n * NB + t + 1)
                act.activation(gbuf[:, gs, s:s + m], ps[:, 6 + t % 2, 0:m], ACT.Gelu,
                               bias=b1_col[:, b, :]).then_inc(gelu_done, 1)

            def high(m, c, gs, free):
                s, n = chunks[c]
                act.wait_ge(mul_done, m + 1)
                if free:
                    act.wait_ge(down_done, m + 1 - 2 * NG)
                act.activation(g_hi[:, gs, s:s + n], gbuf[:, gs, s:s + n], ACT.Copy).then_inc(hi_done, 1)

            def step(n, gs, first, early, q=None):
                b = n if q is None else q
                if b % 2 == 0:
                    act.wait_ge(b1_ready, n // 2 + 1 if q is None else 2 * i + q // 2 + 1)
                for c in range(NG):
                    if not early:
                        act.wait_ge(lo_done, (n - 2) * NG + c + 1)
                    gelu(n, 2 * c, gs, b)
                    gelu(n, 2 * c + 1, gs, b)
                    if c == 0:
                        if not first:
                            high(n * NG - 1, NG - 1, 1 - gs, b >= 3 or q is not None)
                    else:
                        high(n * NG + c - 1, c - 1, gs, not early)

            step(0, 0, True, True)
            step(1, 1, False, True)
            step(2, 0, False, False)
            step(3, 1, False, False)
            with act.Fori(1, HALVES // 4) as i:
                for q in range(4):
                    step(4 * i + q, q % 2, False, False, q)
            high(HALVES * NG - 1, NG - 1, 1, True)
            for t in range(NB):
                s, n = blocks[t]
                act.wait_ge(s_acc, t + 1)
                act.activation(yT[:, s:s + n], ps[:, t, 0:n], ACT.Copy).then_inc(s_y, 1)
            for c in range(PAIRS // 4):
                act.wait_ge(s_yt, c + 1)
                act.activation(y_st[0:PN, 4 * c:4 * c + 4, :], ps[0:PN, 6 + c % 2, :].rearrange("p (a d) -> p a d", a=4),
                               ACT.Copy).then_inc(s_yst, 1)

        @block.vector
        def _(dve):
            with dve.Fori(0, GROUPS) as g:
                for p in range(GP):
                    dve.wait_ge(s_xt, g * XT_STEPS + 2 * p + 2)
                    dve.wait_ge(s_xt_out, g * XT_STEPS + 2 * p + 1)
                    dve.tensor_copy(xT[:, 4:8, p, :],
                                    ps[:, (2 * p + 1) % 4, 0:4 * PM].rearrange("p (r m) -> p r m", r=4)).then_inc(s_xt_out, 1)

            def layer_norm(a):
                def centre(g, slot):
                    dve.wait_ge(ln[a]["mean"], g + 1)
                    dve.tensor_tensor(xc[:, slot, :], hT[:, bass.ds(g * GN, GN)], ps[:, slot, 0:GN],
                                      ALU.subtract).then_inc(ln[a]["xc"], 1)

                def scale(g, slot):
                    dve.wait_ge(ln[a]["sd"], g + 1)
                    dve.reciprocal(sq[:, slot, :], sq[:, slot, :]).then_inc(ln[a]["rs"], 1)
                    dve.wait_ge(ln[a]["rs"], g + 1)
                    dve.tensor_tensor(xn[:, bass.ds(g * GN, GN)], xc[:, slot, :], sq[:, slot, :],
                                      ALU.mult).then_inc(ln[a]["xn"], 1)

                centre(0, 0)
                centre(1, 1)
                with dve.Fori(0, GROUPS // 2 - 1) as j:
                    for s in range(2):
                        scale(2 * j + s, s)
                        dve.wait_ge(ln[a]["xn"], 2 * j + s + 1)
                        centre(2 * j + 2 + s, s)
                for s in range(2):
                    scale(GROUPS - 2 + s, s)

            layer_norm(0)
            dve.wait_ge(s_const, 12)
            dve.wait_ge(ln[0]["xn"], GROUPS)

            def mask(i, s):
                dve.wait_ge(at_s["q"], i + 1)
                for b in range(2):
                    src = ps[:, s, PN:2 * PN].rearrange("p (n b) -> p b n", b=2)[:, b:b + 1, :]
                    op = dve.tensor_tensor(k_blk[:, s, b, :, :], src.to_broadcast([P, HEADS, N]),
                                           head_mask[:, :].rearrange("p (h a) -> p h a", a=1).to_broadcast([P, HEADS, N]),
                                           ALU.mult)
                op.then_inc(at_s["k"], 1)
                dve.wait_ge(at_s["v"], i + 1)
                for b in range(2):
                    op = dve.tensor_tensor(v_blk[0:PN, s, b, :].rearrange("p (c d) -> p c d", c=4),
                                           ps[0:PN, 2 + s, b * D:(b + 1) * D].rearrange("p (c d) -> p c d", c=4),
                                           parity_mask[:, :, :].rearrange("p (o u) d -> p o (u d)", o=1)
                                           .to_broadcast([PN, 4, 2 * HD]), ALU.mult)
                op.then_inc(at_s["vm"], 1)

            def soften(i, s, first):
                sc = ps[:, 4 + s, 0:HEADS * N].rearrange("p (h n) -> p h n", h=HEADS)
                dve.wait_ge(at_s["s"], i + 1)
                dve.reduce_max(smax[:, s, :], sc, AX_X).then_inc(at_s["mx"], 1)
                if not first:
                    dve.wait_ge(at_s["t"], i - 1)
                dve.wait_ge(at_s["mx"], i + 1)
                dve.tensor_tensor(prob[:, s, :, :], sc,
                                  smax[:, s, :].rearrange("p (h a) -> p h a", a=1).to_broadcast([P, HEADS, N]),
                                  ALU.subtract).then_inc(at_s["sub"], 1)
                dve.wait_ge(at_s["exp"], i + 1)
                dve.reduce_sum(ssum[:, s, :], prob[:, s, :, :], AX_X).then_inc(at_s["sum"], 1)
                dve.wait_ge(at_s["sum"], i + 1)
                dve.reciprocal(ssum[:, s, :], ssum[:, s, :]).then_inc(at_s["rec"], 1)
                dve.wait_ge(at_s["rec"], i + 1)
                dve.tensor_tensor(prob[:, s, :, :], prob[:, s, :, :],
                                  ssum[:, s, :].rearrange("p (h a) -> p h a", a=1).to_broadcast([P, HEADS, N]),
                                  ALU.mult).then_inc(at_s["p"], 1)

            def residual(i):
                dve.wait_ge(at_s["pr"], i + 1)
                own = hT[:, bass.ds(i * PN, PN)]
                dve.scalar_tensor_tensor(out=own, in0=ps[:, 7, 256:256 + PN], scalar=bias_cols[:, 1:2], in1=own,
                                         op0=ALU.add, op1=ALU.add).then_inc(at_s["res"], 1)

            mask(0, 0)
            soften(0, 0, True)
            mask(1, 1)
            soften(1, 1, True)
            residual(0)
            with dve.Fori(1, PAIRS // 2) as j:
                mask(2 * j, 0)
                soften(2 * j, 0, False)
                residual(2 * j - 1)
                mask(2 * j + 1, 1)
                soften(2 * j + 1, 1, False)
                residual(2 * j)
            residual(PAIRS - 1)

            layer_norm(1)

            dve.wait_ge(r_s["xh"], 1)
            dve.tensor_tensor(x_lo[:, :], xn, x_hi[:, :].bitcast(F32), ALU.subtract).then_inc(r_s["xh"], 1)

            count = [0]

            def chain(op):
                count[0] += 1
                op.then_inc(r_s["dve"], 1)

            def chained():
                dve.wait_ge(r_s["dve"], count[0])

            def wide(v):
                return v.rearrange("p (t a) -> p t a", a=1).to_broadcast([P, TILES, E])

            logits = ps[:, 0:3, :].rearrange("p b (t e) -> p (b t) e", e=E)[:, 0:TILES, :]
            dve.wait_ge(r_s["lg"], 1)
            chain(dve.reduce_max(rmax, logits, AX_X))
            chained()
            chain(dve.tensor_tensor(rp, logits, wide(rmax), ALU.subtract))
            dve.wait_ge(r_s["act"], 1)
            chain(dve.reduce_sum(rsum, rp, AX_X))
            chained()
            chain(dve.reciprocal(rsum, rsum))
            chained()
            chain(dve.tensor_tensor(rp, rp, wide(rsum), ALU.mult))
            chained()
            chain(dve.reduce_max(pmax, rp, AX_X))
            chained()
            chain(dve.tensor_tensor(re, rp, wide(pmax), ALU.subtract))
            chain(dve.tensor_scalar(rs[:, :, ::-1], rp, -1.0, None, ALU.mult))
            chained()
            for rnd in range(ROUNDS):
                for t in range(TILES):
                    op = dve.max(rtop[:, t, :], rs[:, t, :])
                chain(op)
                chained()
                if rnd == ROUNDS - 1:
                    chain(dve.memset(rtop[:, :, LASTDROP:8], TAKEN))
                    chained()
                for t in range(TILES):
                    op = dve.match_replace(rs[:, t, :], rtop[:, t, :], rs[:, t, :], TAKEN)
                chain(op)
                chained()
            dve.wait_ge(r_s["act"], 2)
            chain(dve.scalar_tensor_tensor(out=re, in0=rs[:, :, ::-1], scalar=TAKEN / 2 - 0.5, in1=re,
                                           op0=ALU.is_gt, op1=ALU.mult))
            chained()
            chain(dve.reduce_sum(rsum, re, AX_X))
            chained()
            chain(dve.reciprocal(rsum, rsum))
            chained()
            chain(dve.tensor_tensor(re, re, wide(rsum), ALU.mult))
            assert count[0] == RDVE

            def mul(m, c, gs, cs, loaded):
                s, n = chunks[c]
                if loaded is not None:
                    dve.wait_ge(c_loaded[cs], loaded)
                dve.wait_ge(gelu_done, 2 * m + 2)
                dve.tensor_tensor(gbuf[:, gs, s:s + n], gbuf[:, gs, s:s + n], cbuf[:, cs, s:s + n],
                                  ALU.mult).then_inc(mul_done, 1)

            def low(m, c, gs):
                s, n = chunks[c]
                dve.wait_ge(hi_done, m + 1)
                dve.tensor_tensor(g_lo[:, gs, s:s + n], gbuf[:, gs, s:s + n], g_hi[:, gs, s:s + n].bitcast(F32),
                                  ALU.subtract).then_inc(lo_done, 1)

            def hidden_biases(e, slot):
                dve.tensor_tensor(b1_col[:, 2 * slot:2 * slot + 2, 0], b1T[:, bass.ds(2 * e, 2)], zeros2[:, 0:2],
                                  ALU.add).then_inc(b1_ready, 1)

            def step(n, q, loaded, first, e=None):
                for c in range(NG):
                    if c == 1 and q % 2 == 0 and e is not None:
                        hidden_biases(e + 1, 1 - q // 2)
                    mul(n * NG + c, c, q % 2, q // 2, loaded if c == 0 and q % 2 == 0 else None)
                    if c:
                        low(n * NG + c - 1, c - 1, q % 2)
                    elif not first:
                        low(n * NG - 1, NG - 1, 1 - q % 2)

            dve.wait_ge(s_b1, 1)
            hidden_biases(0, 0)
            for n in range(4):
                step(n, n, 16, n == 0, n // 2)
            with dve.Fori(1, HALVES // 4 - 1) as i:
                for q in range(4):
                    step(4 * i + q, q, 16 * i + 16, False, 2 * i + q // 2)
            for q in range(4):
                n = HALVES - 4 + q
                step(n, q, 16 * (n // 4) + 16, False, n // 2 if q < 2 else None)
            low(HALVES * NG - 1, NG - 1, 1)


RDVE = 8 + 7 + 4


_INS = ["x", "L0_tok_W", "L0_tok_b", "L0_attn_w_qkv", "L0_attn_w_out", "L0_attn_b_out", "L0_ffn_w1", "L0_ffn_b1",
        "L0_ffn_w2", "L0_ffn_b2", "L0_ffn_router_w", "L0_ffn_router_b"]


def kernel(**inputs):
    import numpy as np
    import concourse.bacc as bacc
    from concourse.bass_utils import run_bass_kernel_spmd

    nc = bacc.Bacc("TRN2", target_bir_lowering=False, num_devices=1)
    arrays, args = {}, []
    for name in _INS:
        a = np.ascontiguousarray(inputs[name])
        arrays[f"in_{name}"] = a
        args.append(nc.dram_tensor(f"in_{name}", a.shape, mybir.dt.from_np(a.dtype), kind="ExternalInput").ap())
    clips, frames, width = arrays["in_x"].shape
    patches = -(-(frames - PATCH) // STRIDE) + 1
    y = nc.dram_tensor("out_y", (clips, patches, width), F32, kind="ExternalOutput").ap()
    audio_tower(nc, *args, y)
    r = run_bass_kernel_spmd(nc, [arrays], core_ids=[0])
    return r.results[0]["out_y"]
```

```python
from contextlib import ExitStack

import concourse.bass as bass
from concourse import mybir

ALU = mybir.AluOpType
ACT = mybir.ActivationFunctionType
F32 = mybir.dt.float32
F32R = mybir.dt.float32r
AX_X = mybir.AxisListType.X

P = 128
EPS = 1e-5
PATCH, STRIDE = 16, 8
HEADS = 8
TOPK = 42
TAKEN = -2.0


def audio_tower(nc, x, tok_W, tok_b, w_qkv, w_out, b_out, w1, b1, w2, b2, router_w, router_b, out):
    B, T, D = x.shape
    E, _, H = w1.shape
    N = out.shape[1]
    M = N + 1
    HD = D // HEADS
    SCALE = float(HD) ** -0.5
    PAIRS = B // 2
    PN, PM = 2 * N, 2 * M
    TOK = B * N
    GP = 4
    GROUPS = PAIRS // GP
    GN = GP * PN
    TILES = TOK // P
    assert D == P and TOK % P == 0 and H == 2 * P and E * 2 == P and PATCH == 2 * STRIDE

    BLK = 512
    blocks = [(s, min(BLK, TOK - s)) for s in range(0, TOK, BLK)]
    NB = len(blocks)
    NG = NB // 2
    chunks = [(blocks[2 * c][0], blocks[2 * c][1] + blocks[2 * c + 1][1]) for c in range(NG)]
    HALVES = 2 * E
    DROP = E - TOPK
    ROUNDS = -(-DROP // 8)
    LASTDROP = DROP - 8 * (ROUNDS - 1)

    comb_dram = nc.dram_tensor("comb_scratch", (E, TOK), F32).ap()

    with ExitStack() as ctx:
        def sb(name, shape, dt=F32):
            return ctx.enter_context(nc.sbuf_tensor(name, shape, dt))

        def sem(name):
            return ctx.enter_context(nc.semaphore(name))

        ps = ctx.enter_context(nc.psum_tensor("ps", [P, 8, BLK], F32))

        ident = sb("ident", [P, P])
        ones_mean = sb("ones_mean", [P, P])
        ones_row = sb("ones_row", [1, P])
        eps_col = sb("eps_col", [P, 1])
        head_mask = sb("head_mask", [P, HEADS])
        parity_mask = sb("parity_mask", [PN, 2, HD])
        W_raw = sb("W_raw", [P, D * PATCH])
        bias_cols = sb("bias_cols", [P, 2])
        wqkv_sb = sb("wqkv_sb", [P, 3 * D])
        wout_sb = sb("wout_sb", [P, D])
        rw_sb = sb("rw_sb", [P, E])
        rb_sb = sb("rb_sb", [1, E])
        b1_raw = sb("b1_raw", [P, P])
        b1T = sb("b1T", [P, HALVES])
        b2_sb = sb("b2_sb", [E, D])
        b1_col = sb("b1_col", [P, 4, 1])
        zeros2 = sb("zeros2", [P, 4])
        pool_tick = sb("pool_tick", [P, 1])

        hT = sb("hT", [P, TOK])

        xn = sb("xn", [P, TOK])[:, :]

        gbuf = sb("gbuf", [P, 2, TOK])
        cbuf = sb("cbuf", [P, 2, TOK])
        SLOT = max(TOK, STRIDE * GP * PM)
        parts_hi = sb("parts_hi", [P, 2 * SLOT], F32R)
        parts_lo = sb("parts_lo", [P, 2 * SLOT], F32R)
        g_hi = parts_hi[:, 0:2 * TOK].rearrange("p (s n) -> p s n", s=2)
        g_lo = parts_lo[:, 0:2 * TOK].rearrange("p (s n) -> p s n", s=2)
        x_hi = sb("x_hi", [P, TOK], F32R)
        x_lo = sb("x_lo", [P, TOK], F32R)
        w_raw = sb("w_raw", [P, 2, 2 * H])
        w_hi = sb("w_hi", [P, 2, 2 * H], F32R)
        w_lo = sb("w_lo", [P, 2, 2 * H], F32R)

        gflat = gbuf[:, :, :].rearrange("p a b -> p (a b)")
        cflat = cbuf[:, :, :].rearrange("p a b -> p (a b)")
        xin = gflat[:, 0:GP * STRIDE * D].rearrange("p (a b) -> p a b", a=GP)
        XTN = STRIDE * GP * PM
        xT_hi = parts_hi[:, 0:2 * XTN].rearrange("p (s r a m) -> p s r a m", s=2, r=STRIDE, a=GP)
        xT_lo = parts_lo[:, 0:2 * XTN].rearrange("p (s r a m) -> p s r a m", s=2, r=STRIDE, a=GP)
        WT_hi = x_hi[:, 0:PATCH * P].rearrange("p (f e) -> p f e", f=PATCH)
        WT_lo = x_lo[:, 0:PATCH * P].rearrange("p (f e) -> p f e", f=PATCH)
        LN0 = 2 * TOK - 4 * GN
        xc = cflat[:, LN0:LN0 + 2 * GN].rearrange("p (s n) -> p s n", s=2)
        sq = cflat[:, LN0 + 2 * GN:LN0 + 4 * GN].rearrange("p (s n) -> p s n", s=2)
        at = [0]

        def carve(cols):
            at[0] += cols
            return cflat[:, at[0] - cols:at[0]]

        q_st = carve(2 * 128).rearrange("p (s b n) -> p s b n", s=2, b=2)
        x_st = carve(2 * 4 * N).rearrange("p (s b c n) -> p s b c n", s=2, b=2, c=2)
        k_blk = carve(4 * HEADS * N).rearrange("p (s b h n) -> p s b h n", s=2, b=2, h=HEADS)
        v_blk = carve(8 * D).rearrange("p (s b d) -> p s b d", s=4, b=2)
        prob = carve(2 * HEADS * N).rearrange("p (s h n) -> p s h n", s=2, h=HEADS)
        pT = carve(8 * P).rearrange("p (s c n) -> p s c n", s=2, c=4)
        assert at[0] <= 2 * TOK
        o_st = gflat[:, 0:2 * PN].rearrange("p (s n) -> p s n", s=2)
        o_rec = gflat[:, 2 * PN:3 * PN]
        smax = gflat[:, 320:320 + 2 * HEADS].rearrange("p (s h) -> p s h", s=2)
        xc2, sq2 = (gflat[:, TOK + k * GN:TOK + (k + 1) * GN] for k in range(2))
        RW = TILES * E
        rp = cflat[:, 0:RW].rearrange("p (t e) -> p t e", e=E)
        re = cflat[:, RW:2 * RW].rearrange("p (t e) -> p t e", e=E)
        rs = cflat[:, 2 * RW:3 * RW].rearrange("p (t e) -> p t e", e=E)
        rtop = cflat[:, 3 * RW:3 * RW + 8 * TILES].rearrange("p (t k) -> p t k", k=8)
        rmax, rinv, rneg, rsum = (cflat[:, 3 * RW + (8 + k) * TILES:3 * RW + (9 + k) * TILES] for k in range(4))
        combT = gbuf[0:E, 1, :]
        yT = gflat[:, 0:TOK]
        y_st = cflat[:, 0:TOK].rearrange("p (t d) -> p t d", d=D)

        s_const = sem("s_const")
        s_bias = sem("s_bias")
        s_small = sem("s_small")
        s_wraw = sem("s_wraw")
        s_wt = sem("s_wt")
        s_wt_hi = sem("s_wt_hi")
        s_wt_lo = sem("s_wt_lo")
        s_xzero = sem("s_xzero")
        s_xin = [sem(f"s_xin{p}") for p in range(GP)]
        s_xt = sem("s_xt")
        s_xt_hi = sem("s_xt_hi")
        s_xt_lo = sem("s_xt_lo")
        s_tok = sem("s_tok")
        s_tok_out = sem("s_tok_out")
        ln = [{k: sem(f"s_ln{a}_{k}") for k in ("mean", "xc", "sq", "var", "sd", "rs", "xn")} for a in range(2)]
        for k in ("sd", "xn"):
            ln[1][k] = ln[0][k]
        at_s = {k: sem(f"s_at_{k}") for k in ("xst", "qk", "q", "k", "vm", "s", "mx", "sub", "exp", "t", "pt", "o", "rec",
                                              "ost", "pr", "res", "zero")}
        r_s = {k: sem(f"s_r_{k}") for k in ("xh", "lg", "dve", "act", "neg", "t", "ct", "dram", "b2")}
        s_b1t = sem("s_b1t")
        s_b1 = sem("s_b1")
        w_loaded = [sem(f"w_loaded{s}") for s in range(2)]
        c_loaded = [sem(f"c_loaded{s}") for s in range(2)]
        s_acc = sem("s_acc")
        w_split = sem("w_split")
        s_tick = sem("s_tick")
        b1_ready = sem("b1_ready")
        w_hi_done = sem("w_hi_done")
        up_done = sem("up_done")
        gelu_done = sem("gelu_done")
        mul_done = sem("mul_done")
        hi_done = sem("hi_done")
        lo_done = sem("lo_done")
        down_done = sem("down_done")
        s_y = sem("s_y")
        s_yt = sem("s_yt")
        s_yst = sem("s_yst")
        s_out = sem("s_out")

        LAG = 4

        def runs(t, lag):
            return t is None or lag <= t < PAIRS + lag

        def turns(eng, attend, norm):
            for t in range(2 * GP):
                attend(t, t % 4, t)
            with eng.Fori(2, GROUPS) as j:
                for q in range(4):
                    attend(4 * j + q, q)
                    norm(j - 2, q)
            for t in range(PAIRS, PAIRS + LAG):
                attend(t, t % 4, t)
                norm(GROUPS - 2, t % 4)
            for q in range(4):
                norm(GROUPS - 1, q)

        block = ctx.enter_context(nc.Block())

        OUT_TILES = [(t, min(t + 4, TILES)) for t in range(0, TILES, 4)]
        XT_STEPS = 2 * GP
        EX2 = E // 2 - 1

        @block.sync
        def _(sp):
            nc_ = sp
            nc_.dma_start(W_raw[:, :], tok_W).then_inc(s_wraw, 16)
            sp.wait_ge(s_xzero, 1)

            SPLIT = 32

            def frames(g, p):
                pair = g * GP + p
                rows = x[bass.ds(2 * pair, 2), 0:N * STRIDE, :].rearrange("b (m r) d -> m b (r d)", r=STRIDE)
                sp.dma_start(xin[0:2 * SPLIT, p, :], rows[0:SPLIT, :, :]).then_inc(s_xin[p], 16)
                sp.dma_start(xin[2 * SPLIT:PN, p, :], rows[SPLIT:N, :, :]).then_inc(s_xin[p], 16)
                rest = x[bass.ds(2 * pair, 2), N * STRIDE:T, :].rearrange("b r d -> b (r d)")
                sp.dma_start(xin[PN:PM, p, 0:(T - N * STRIDE) * D], rest).then_inc(s_xin[p], 16)

            for p in range(GP):
                frames(0, p)
            small = [(bias_cols[:, 0:1], tok_b.rearrange("(p a) -> p a", a=1)),
                     (bias_cols[:, 1:2], b_out.rearrange("(p a) -> p a", a=1)),
                     (wqkv_sb[:, :], w_qkv), (wout_sb[:, :], w_out), (rw_sb[:, :], router_w),
                     (rb_sb[:, :], router_b.rearrange("(a e) -> a e", a=1)),
                     (b1_raw[:, :], b1.rearrange("e (j h) -> (e j) h", j=2)), (b2_sb[:, :], b2)]
            for dst, src in small:
                sp.dma_start(dst, src).then_inc(s_small, 16)
            with sp.Fori(1, GROUPS) as g:
                for p in range(GP):
                    sp.wait_ge(s_xt, (g - 1) * XT_STEPS + 2 * p + 2)
                    frames(g, p)

            def weights(e, slot):
                sp.dma_start(w_raw[:, slot, 0:H], w1[bass.ds(e, 1), :, :].rearrange("a d h -> d (a h)")).then_inc(w_loaded[slot], 16)
                sp.dma_start(w_raw[:, slot, H:2 * H].rearrange("p (j d) -> p j d", j=2),
                             w2[bass.ds(e, 1), :, :].rearrange("a (j p) d -> p (a j) d", j=2)).then_inc(w_loaded[slot], 16)

            def combine(e, slot):
                sp.dma_start(cbuf[:, slot, :], comb_dram[bass.ds(e, 1), :].to_broadcast([P, TOK])).then_inc(c_loaded[slot], 16)

            for e in range(2):
                weights(e, e)
            sp.wait_ge(r_s["t"], TILES)
            sp.wait_ge(r_s["ct"], NB)
            sp.dma_start(comb_dram, combT).then_inc(r_s["dram"], 16)
            sp.wait_ge(r_s["dram"], 16)
            for e in range(2):
                combine(e, e)
            with sp.Fori(0, EX2) as i:
                for slot in range(2):
                    sp.wait_ge(w_split, 2 * i + slot + 1)
                    weights(2 * i + 2 + slot, slot)
                    sp.wait_ge(mul_done, (2 * i + slot + 1) * 2 * NG)
                    combine(2 * i + 2 + slot, slot)

            rows = out.rearrange("b n d -> (b n) d").rearrange("(t p) d -> p t d", p=P)
            for c, (t0, t1) in enumerate(OUT_TILES):
                sp.wait_ge(s_yst, c + 1)
                sp.dma_start(rows[:, t0:t1, :], y_st[:, t0:t1, :]).then_inc(s_out, 16)
            sp.wait_ge(s_out, 16 * len(OUT_TILES))

        @block.gpsimd
        def _(pool):
            pool.memset(gflat[:, 0:GP * STRIDE * D], 0.0).then_inc(s_xzero, 1)
            pool.memset(pool_tick[:, :], 0.0).then_inc(s_tick, 1)
            pool.memset(ident[:, :], 0.0).then_inc(s_const, 1)
            pool.memset(ones_mean[:, :], 1.0 / D).then_inc(s_const, 1)
            pool.memset(ones_row[:, :], 1.0).then_inc(s_const, 1)
            pool.memset(eps_col[:, :], EPS).then_inc(s_const, 1)
            pool.memset(head_mask[:, :], 1.0).then_inc(s_const, 1)
            pool.memset(parity_mask[:, :, :], 1.0).then_inc(s_const, 1)
            pool.memset(zeros2[:, :], 0.0).then_inc(s_const, 1)
            pool.wait_ge(s_const, 7)
            pool.affine_select(out=ident[:, :], in_=ident[:, :], compare_op=ALU.not_equal, fill=1.0, base=0,
                               pattern=[[-1, P]], channel_multiplier=1).then_inc(s_const, 1)
            pool.affine_select(out=head_mask[:, :], in_=head_mask[:, :], compare_op=ALU.is_ge, fill=0.0, base=0,
                               pattern=[[-HD, HEADS]], channel_multiplier=1).then_inc(s_const, 1)
            pool.affine_select(out=parity_mask[:, 0, :], in_=parity_mask[:, 0, :], compare_op=ALU.is_ge, fill=0.0,
                               base=N - 1, pattern=[[0, HD]], channel_multiplier=-1).then_inc(s_const, 1)
            pool.affine_select(out=parity_mask[:, 1, :], in_=parity_mask[:, 1, :], compare_op=ALU.is_ge, fill=0.0,
                               base=-N, pattern=[[0, HD]], channel_multiplier=1).then_inc(s_const, 1)
            pool.wait_ge(s_const, 11)
            pool.affine_select(out=head_mask[:, :], in_=head_mask[:, :], compare_op=ALU.is_ge, fill=0.0, base=HD - 1,
                               pattern=[[HD, HEADS]], channel_multiplier=-1).then_inc(s_const, 1)
            pool.wait_ge(ln[0]["xn"], GROUPS)
            pool.memset(q_st[:, :, :, :], 0.0).then_inc(at_s["zero"], 1)

            def stage(i, s):
                if s is not None:
                    src = xn[:, bass.ds(i * PN, PN)].rearrange("p (n b) -> p b n", b=2)
                    for c in range(2):
                        pool.tensor_copy(x_st[:, s, :, c, :], src).then_inc(at_s["xst"], 1)

            for s in range(2):
                stage(s, s)
            with pool.Fori(0, PAIRS // 2 - 1) as j:
                for s in range(2):
                    pool.wait_ge(at_s["qk"], 2 * j + s + 1)
                    stage(2 * j + 2 + s, s)

            pool.wait_ge(r_s["xh"], 1)
            pool.tensor_tensor(x_lo[:, :], xn, x_hi[:, :].bitcast(F32), ALU.subtract).then_inc(r_s["xh"], 1)

            def split(e, slot, use):
                first = isinstance(use, int)
                pool.wait_ge(w_loaded[slot], 32 * (use + 1))
                if not first:
                    pool.wait_ge(s_tick, e - 1)
                    pool.wait_ge(down_done, (e - 1) * 2 * NG)
                    pool.tensor_tensor(pool_tick[:, :], eps_col[:, :], eps_col[:, :], ALU.add).then_inc(s_tick, 1)
                pool.tensor_copy(w_hi[:, slot, :], w_raw[:, slot, :]).then_inc(w_hi_done, 1)
                pool.wait_ge(w_hi_done, e + 1)
                pool.tensor_tensor(w_lo[:, slot, :], w_raw[:, slot, :], w_hi[:, slot, :].bitcast(F32),
                                   ALU.subtract).then_inc(w_split, 1)

            for e in range(2):
                split(e, e, 0)
            with pool.Fori(0, EX2) as i:
                for slot in range(2):
                    split(2 * i + 2 + slot, slot, i + 1)

        @block.tensor
        def _(pe):
            pe.wait_ge(s_const, 12)
            pe.wait_ge(s_wraw, 16)
            Wv = W_raw[:, :].rearrange("e (d f) -> e f d", f=PATCH)
            for f in range(PATCH):
                mm = pe.transpose(ps[:, 4 + f // 4, f % 4 * P:(f % 4 + 1) * P], Wv[:, f, :], ident[:, :])
                if f % 4 == 3:
                    mm.then_inc(s_wt, 1)

            def transpose_frames(g, k, first):
                p, half = k // 2, k % 2
                if half == 0:
                    pe.wait_ge(s_xin[p], 48 * (g + 1))
                if not (first and k < 4):
                    pe.wait_ge(s_xt_lo, g * XT_STEPS + k - 3)
                for c in range(4):
                    r = 4 * half + c
                    mm = pe.transpose(ps[:, k % 4, c * PM:(c + 1) * PM], xin[0:PM, p, r * D:(r + 1) * D],
                                      ident[0:PM, 0:PM])
                mm.then_inc(s_xt, 1)

            def embed(g, f, slot):
                r, s = f % STRIDE, f // STRIDE
                hi = xT_hi[:, slot, r, :, 2 * s:2 * s + PN]
                lo = xT_lo[:, slot, r, :, 2 * s:2 * s + PN]
                o = ps[:, 4 + slot, 0:GN]
                pe.matmul(o, WT_hi[:, f, :], lo, start=(f == 0), stop=False)
                pe.matmul(o, WT_lo[:, f, :], hi, start=False, stop=False)
                mm = pe.matmul(o, WT_hi[:, f, :], hi, start=False, stop=(f == PATCH - 1))
                if f == PATCH - 1:
                    mm.then_inc(s_tok, 1)

            def mean1(g):
                pe.wait_ge(s_tok_out, g + 1)
                pe.matmul(ps[:, 6, 0:GN], ones_mean[:, :], hT[:, bass.ds(g * GN, GN)],
                          start=True, stop=True).then_inc(ln[0]["mean"], 1)

            def var1(g, slot):
                pe.wait_ge(ln[0]["sq"], g + 1)
                pe.matmul(ps[:, 7, 0:GN], ones_mean[:, :], sq[:, slot, :],
                          start=True, stop=True).then_inc(ln[0]["var"], 1)

            def tokens(g, slot, last=False, first=False):
                pe.wait_ge(s_xt_lo, (g + 1) * XT_STEPS)
                for k in range(XT_STEPS):
                    if not last:
                        transpose_frames(g + 1, k, False)
                    for f in range(2 * k, 2 * k + 2):
                        embed(g, f, slot)
                    if k == 1 and not first:
                        mean1(g - 1)
                    if k == 5 and not first:
                        var1(g - 1, 1 - slot)

            for k in range(XT_STEPS):
                transpose_frames(0, k, True)
            pe.wait_ge(s_wt_lo, 4)
            tokens(0, 0, first=True)
            with pe.Fori(0, GROUPS // 2 - 1) as j:
                tokens(2 * j + 1, 1)
                tokens(2 * j + 2, 0)
            tokens(GROUPS - 1, 1, last=True)
            mean1(GROUPS - 1)
            var1(GROUPS - 1, 1)

            pe.wait_ge(s_small, 16 * 8)
            pe.wait_ge(ln[0]["xn"], GROUPS)

            def project_in(i, s, first):
                tok = xn[:, bass.ds(i * PN, PN)]
                if not first:
                    pe.wait_ge(at_s["k"], i - 1)
                pe.matmul(ps[:, s, 0:PN], wqkv_sb[:, 0:D], tok, start=True, stop=True)
                pe.matmul(ps[:, s, PN:2 * PN], wqkv_sb[:, D:2 * D], tok, start=True, stop=True)
                pe.wait_ge(at_s["xst"], 2 * i + 2)
                for b in range(2):
                    mm = pe.matmul(ps[0:PN, s, 2 * PN + b * D:2 * PN + (b + 1) * D], x_st[:, s, b, :, :],
                                   wqkv_sb[:, 2 * D:3 * D], start=True, stop=True)
                mm.then_inc(at_s["qk"], 1)

            def scores(i, s, first):
                pe.wait_ge(at_s["k"], i + 1)
                if not first:
                    pe.wait_ge(at_s["sub"], i - 1)
                for b in range(2):
                    mm = pe.matmul(ps[64 * b:64 * b + 64, 2 + s, 0:HEADS * N], q_st[:, s, b, :], k_blk[:, s, b, :, :],
                                   start=True, stop=True)
                mm.then_inc(at_s["s"], 1)

            def flip(i, s, first):
                pe.wait_ge(at_s["exp"], i + 1)
                if not first:
                    pe.wait_ge(at_s["pt"], i)
                for c in range(4):
                    mm = pe.transpose(ps[0:PN, 4, c * P:(c + 1) * P], prob[:, s, 2 * c:2 * c + 2, :], ident[:, :])
                mm.then_inc(at_s["t"], 1)

            def weigh(i, s, vs, first):
                pe.wait_ge(at_s["pt"], i + 1)
                if not first:
                    pe.wait_ge(at_s["ost"], i)
                for c in range(4):
                    for b in range(2):
                        rows, cols, p_bc = slice(32 * c, 32 * c + 32), slice(b * N, (b + 1) * N), pT[0:PN, s, c, 64 * b:64 * b + N]
                        pe.matmul(ps[rows, 5, cols], v_blk[0:PN, vs, b, rows], p_bc, start=True, stop=True)
                        mm = pe.matmul(ps[rows, 5, 128 + b * N:128 + (b + 1) * N], parity_mask[0:PN, :, :], p_bc,
                                       start=True, stop=True)
                mm.then_inc(at_s["o"], 1)

            def project_out(i, s, first):
                pe.wait_ge(at_s["ost"], i + 1)
                if not first:
                    pe.wait_ge(at_s["res"], i)
                pe.matmul(ps[:, 6, 0:PN], wout_sb[:, :], o_st[:, s, :], start=True, stop=True).then_inc(at_s["pr"], 1)

            def attend(i, q, t=None):
                if runs(t, 0):
                    project_in(i, q % 2, t in (0, 1))
                if runs(t, 4):
                    project_out(i - 4, q % 2, t == 4)
                if runs(t, 1):
                    scores(i - 1, (q - 1) % 2, t in (1, 2))
                if runs(t, 3):
                    weigh(i - 3, (q - 3) % 2, (q - 3) % 4, t == 3)
                if runs(t, 2):
                    flip(i - 2, q % 2, t == 2)

            def norm(g, q):
                if q == 0:
                    pe.wait_ge(at_s["res"], GP * (g + 1))
                    pe.wait_ge(ln[1]["sd"], GROUPS + g)
                    pe.matmul(ps[:, 7, 0:GN], ones_mean[:, :], hT[:, bass.ds(g * GN, GN)],
                              start=True, stop=True).then_inc(ln[1]["mean"], 1)
                if q == 2:
                    pe.wait_ge(ln[1]["sq"], g + 1)
                    pe.matmul(ps[:, 7, 0:GN], ones_mean[:, :], sq2, start=True, stop=True).then_inc(ln[1]["var"], 1)

            turns(pe, attend, norm)

            pe.wait_ge(ln[1]["xn"], 2 * GROUPS)
            for c in range(0, TILES, 8):
                n = min(8, TILES - c)
                pe.matmul(ps[:, c // 8, 0:n * E], ones_row[:, :], rb_sb[:, :].rearrange("p (a e) -> p a e", a=1)
                          .to_broadcast([1, n, E]), start=True, stop=False, skip_group_check=True)
                for t in range(c, c + n):
                    mm = pe.matmul(ps[:, c // 8, (t - c) * E:(t - c + 1) * E], xn[:, t * P:(t + 1) * P], rw_sb[:, :],
                                   start=False, stop=(t == c + n - 1), skip_group_check=True)
            mm.then_inc(r_s["lg"], 1)
            pe.transpose(ps[:, 3, 0:P], b1_raw[:, :], ident[:, :]).then_inc(s_b1t, 1)
            def up(k0, t, w, free):
                s, n = blocks[t]
                slot, j = w
                if free:
                    pe.wait_ge(gelu_done, k0 + t - 1)
                cols = slice(j * P, (j + 1) * P)
                o = ps[:, 6 + t % 2, 0:n]
                pe.matmul(o, w_hi[:, slot, cols], x_lo[:, s:s + n], start=True, stop=False)
                pe.matmul(o, w_lo[:, slot, cols], x_hi[:, s:s + n], start=False, stop=False)
                pe.matmul(o, w_hi[:, slot, cols], x_hi[:, s:s + n], start=False, stop=True).then_inc(up_done, 1)

            def down(m0, t, w, gs, last=False):
                s, n = blocks[t]
                slot, j = w
                if t % 2 == 0:
                    pe.wait_ge(lo_done, m0 + t // 2 + 1)
                cols = slice(H + j * P, H + (j + 1) * P)
                o = ps[:, t, 0:n]
                pe.matmul(o, w_hi[:, slot, cols], g_lo[:, gs, s:s + n], start=False, stop=False, skip_group_check=True)
                pe.matmul(o, w_lo[:, slot, cols], g_hi[:, gs, s:s + n], start=False, stop=False, skip_group_check=True)
                mm = pe.matmul(o, w_hi[:, slot, cols], g_hi[:, gs, s:s + n], start=False, stop=last, skip_group_check=True)
                if last:
                    mm.then_inc(s_acc, 1)
                elif t % 2 == 1:
                    mm.then_inc(down_done, 1)

            def step(n, q):
                for t in range(NB):
                    if t == 0 and q % 2 == 0:
                        pe.wait_ge(w_split, (n + 2) // 2 if isinstance(n, int) else n[1])
                    nn = n if isinstance(n, int) else n[0]
                    up(nn * NB, t, (q // 2, q % 2), True)
                    pq = (q - 1) % 4
                    down((nn - 1) * NG, t, (pq // 2, pq % 2), pq % 2)

            pe.wait_ge(w_split, 1)
            pe.wait_ge(r_s["xh"], 2)
            for t in range(NB):
                up(0, t, (0, 0), t >= 2)

            pe.wait_ge(r_s["dve"], RDVE)
            for t in range(TILES):
                bank = t // 4
                pe.transpose(ps[0:E, bank, t % 4 * P:(t % 4 + 1) * P], re[:, t, :], ident[:, :]).then_inc(r_s["t"], 1)
            pe.wait_ge(r_s["ct"], NB)
            for t, (s, n) in enumerate(blocks):
                mm = pe.matmul(ps[:, t, 0:n], b2_sb[:, :], combT[:, s:s + n], start=True, stop=False, skip_group_check=True)
            mm.then_inc(r_s["b2"], 1)
            with pe.Fori(0, EX2) as i:
                for q in range(4):
                    step((4 * i + 1 + q, 2 * i + (q + 3) // 2), (1 + q) % 4)
            for n in range(4 * EX2 + 1, HALVES):
                step(n, n % 4)
            for t in range(NB):
                down((HALVES - 1) * NG, t, (1, 1), 1, last=True)
            for c, (t0, t1) in enumerate(OUT_TILES):
                pe.wait_ge(s_y, -(-t1 * P // GN))
                if c >= 2:
                    pe.wait_ge(s_yst, c - 1)
                for t in range(t0, t1):
                    mm = pe.transpose(ps[:, 6 + c % 2, (t - t0) * P:(t - t0 + 1) * P], yT[:, t * P:(t + 1) * P], ident[:, :])
                mm.then_inc(s_yt, 1)

        @block.scalar
        def _(act):
            for c in range(4):
                act.wait_ge(s_wt, c + 1)
                act.activation(WT_hi[:, 4 * c:4 * c + 4, :], ps[:, 4 + c, :].rearrange("p (f e) -> p f e", f=4),
                               ACT.Copy).then_inc(s_wt_hi, 1)

            def frames_hi(g, k, slot):
                act.wait_ge(s_xt, g * XT_STEPS + k + 1)
                p, half = k // 2, k % 2
                act.activation(xT_hi[:, slot, 4 * half:4 * half + 4, p, :],
                               ps[:, k % 4, 0:4 * PM].rearrange("p (r m) -> p r m", r=4), ACT.Copy).then_inc(s_xt_hi, 1)

            def tokens_out(g, slot):
                act.wait_ge(s_tok, g + 1)
                act.activation(hT[:, bass.ds(g * GN, GN)], ps[:, 4 + slot, 0:GN], ACT.Identity,
                               bias=bias_cols[:, 0:1]).then_inc(s_tok_out, 1)

            def square1(g, slot):
                act.wait_ge(ln[0]["xc"], g + 1)
                act.activation(sq[:, slot, :], xc[:, slot, :], ACT.Square).then_inc(ln[0]["sq"], 1)

            def root1(g, slot):
                act.wait_ge(ln[0]["var"], g + 1)
                act.activation(sq[:, slot, :], ps[:, 7, 0:GN], ACT.Sqrt, bias=eps_col[:, :]).then_inc(ln[0]["sd"], 1)

            def tokens(g, slot, last=False, first=False):
                if not first:
                    tokens_out(g - 1, 1 - slot)
                for k in range(XT_STEPS):
                    if not last:
                        frames_hi(g + 1, k, 1 - slot)
                    if k == 3 and not first:
                        square1(g - 1, 1 - slot)
                    if k == 6 and not first:
                        root1(g - 1, 1 - slot)

            for k in range(XT_STEPS):
                frames_hi(0, k, 0)
            act.wait_ge(s_small, 16 * 8)
            tokens(0, 0, first=True)
            with act.Fori(0, GROUPS // 2 - 1) as j:
                tokens(2 * j + 1, 1)
                tokens(2 * j + 2, 0)
            tokens(GROUPS - 1, 1, last=True)
            tokens_out(GROUPS - 1, 1)
            square1(GROUPS - 1, 1)
            root1(GROUPS - 1, 1)

            act.wait_ge(at_s["zero"], 1)

            def attend(i, q, t=None):
                if runs(t, 0):
                    act.wait_ge(at_s["qk"], i + 1)
                    s = q % 2
                    act.activation(q_st[:, s, :, 0:N], ps[:, s, 0:PN].rearrange("p (n b) -> p b n", b=2),
                                   ACT.Copy, scale=SCALE)
                    src = ps[0:PN, s, 2 * PN:2 * PN + 2 * D].rearrange("p (c u d) -> p c u d", u=2, d=HD)
                    dst = v_blk[0:PN, q, :, :].rearrange("p b (c u d) -> p (b c) u d", u=2, d=HD)
                    for u in range(2):
                        op = act.activation(dst[:, :, u, :], src[:, :, u, :], ACT.Copy, scale=parity_mask[0:PN, u, 0:1])
                    op.then_inc(at_s["q"], 1)
                if runs(t, 2):
                    act.wait_ge(at_s["t"], i - 1)
                    act.activation(pT[0:PN, q % 2, :, :], ps[0:PN, 4, :].rearrange("p (c n) -> p c n", c=4),
                                   ACT.Copy).then_inc(at_s["pt"], 1)
                if runs(t, 1):
                    act.wait_ge(at_s["sub"], i)
                    s = (q - 1) % 2
                    act.activation(prob[:, s, :, :], prob[:, s, :, :], ACT.Exp).then_inc(at_s["exp"], 1)

            def norm(g, q):
                if q == 1:
                    act.wait_ge(ln[1]["xc"], g + 1)
                    act.activation(sq2, xc2, ACT.Square).then_inc(ln[1]["sq"], 1)
                if q == 2:
                    act.wait_ge(ln[1]["var"], g + 1)
                    act.activation(sq2, ps[:, 7, 0:GN], ACT.Sqrt, bias=eps_col[:, :]).then_inc(ln[1]["sd"], 1)

            turns(act, attend, norm)

            act.wait_ge(ln[1]["xn"], 2 * GROUPS)
            act.activation(x_hi[:, :], xn, ACT.Copy).then_inc(r_s["xh"], 1)
            act.wait_ge(r_s["dve"], 2)
            act.activation(rp, rp, ACT.Exp).then_inc(r_s["act"], 1)
            act.wait_ge(r_s["act"], 1)
            act.activation(rs[:, :, ::-1], rp, ACT.Copy, scale=-1.0).then_inc(r_s["neg"], 1)
            act.wait_ge(s_b1t, 1)
            act.activation(b1T[:, :], ps[:, 3, 0:P], ACT.Copy).then_inc(s_b1, 1)
            act.wait_ge(r_s["dve"], 5)
            for t in range(TILES):
                op = act.activation(re[:, t, :], rp[:, t, :], ACT.Exp, scale=rinv[:, t:t + 1], bias=rneg[:, t:t + 1])
            op.then_inc(r_s["act"], 1)

            def gelu(n, t, gs, b):
                s, m = blocks[t]
                act.wait_ge(up_done, n * NB + t + 1)
                act.activation(gbuf[:, gs, s:s + m], ps[:, 6 + t % 2, 0:m], ACT.Gelu,
                               bias=b1_col[:, b, :]).then_inc(gelu_done, 1)

            def high(m, c, gs, free):
                s, n = chunks[c]
                act.wait_ge(mul_done, m + 1)
                if free:
                    act.wait_ge(down_done, m + 1 - 2 * NG)
                act.activation(g_hi[:, gs, s:s + n], gbuf[:, gs, s:s + n], ACT.Copy).then_inc(hi_done, 1)

            def step(n, gs, first, early, q=None):
                b = n if q is None else q
                if b % 2 == 0:
                    act.wait_ge(b1_ready, n // 2 + 1 if q is None else 2 * i + q // 2 + 1)
                for c in range(NG):
                    if not early:
                        act.wait_ge(lo_done, (n - 2) * NG + c + 1)
                    gelu(n, 2 * c, gs, b)
                    gelu(n, 2 * c + 1, gs, b)
                    if c == 0:
                        if not first:
                            high(n * NG - 1, NG - 1, 1 - gs, b >= 3 or q is not None)
                    else:
                        high(n * NG + c - 1, c - 1, gs, not early)

            act.wait_ge(b1_ready, 1)
            for t in range(NB):
                gelu(0, t, 0, 0)
            for t, (s, n) in enumerate(blocks):
                act.wait_ge(r_s["t"], min(4 * t + 4, TILES))
                act.activation(combT[:, s:s + n], ps[0:E, t, 0:n], ACT.Copy).then_inc(r_s["ct"], 1)
            for c in range(NG - 1):
                high(c, c, 0, False)
            act.wait_ge(r_s["dram"], 16)
            act.wait_ge(r_s["b2"], 1)
            step(1, 1, False, True)
            step(2, 0, False, False)
            step(3, 1, False, False)
            with act.Fori(1, HALVES // 4) as i:
                for q in range(4):
                    step(4 * i + q, q % 2, False, False, q)
            high(HALVES * NG - 1, NG - 1, 1, True)
            for c, (t0, t1) in enumerate(OUT_TILES):
                act.wait_ge(s_yt, c + 1)
                act.activation(y_st[:, t0:t1, :], ps[:, 6 + c % 2, 0:(t1 - t0) * P].rearrange("p (t d) -> p t d", d=D),
                               ACT.Copy).then_inc(s_yst, 1)

        @block.vector
        def _(dve):
            for c in range(4):
                dve.wait_ge(s_wt_hi, c + 1)
                dve.tensor_tensor(WT_lo[:, 4 * c:4 * c + 4, :], ps[:, 4 + c, :].rearrange("p (f e) -> p f e", f=4),
                                  WT_hi[:, 4 * c:4 * c + 4, :].bitcast(F32), ALU.subtract).then_inc(s_wt_lo, 1)

            def frames_lo(g, k, slot):
                dve.wait_ge(s_xt_hi, g * XT_STEPS + k + 1)
                p, half = k // 2, k % 2
                rows = slice(4 * half, 4 * half + 4)
                dve.tensor_tensor(xT_lo[:, slot, rows, p, :], ps[:, k % 4, 0:4 * PM].rearrange("p (r m) -> p r m", r=4),
                                  xT_hi[:, slot, rows, p, :].bitcast(F32), ALU.subtract).then_inc(s_xt_lo, 1)

            def centre1(g, slot):
                dve.wait_ge(ln[0]["mean"], g + 1)
                dve.tensor_tensor(xc[:, slot, :], hT[:, bass.ds(g * GN, GN)], ps[:, 6, 0:GN],
                                  ALU.subtract).then_inc(ln[0]["xc"], 1)

            def inverse1(g, slot):
                dve.wait_ge(ln[0]["sd"], g + 1)
                dve.reciprocal(sq[:, slot, :], sq[:, slot, :]).then_inc(ln[0]["rs"], 1)

            def normal1(g, slot):
                dve.wait_ge(ln[0]["rs"], g + 1)
                dve.tensor_tensor(xn[:, bass.ds(g * GN, GN)], xc[:, slot, :], sq[:, slot, :],
                                  ALU.mult).then_inc(ln[0]["xn"], 1)

            def tokens(g, slot, last=False, first=False, second=False):
                for k in range(XT_STEPS):
                    if not last:
                        frames_lo(g + 1, k, 1 - slot)
                    if k == 0 and not first and not second:
                        inverse1(g - 2, slot)
                    if k == 1 and not first and not second:
                        normal1(g - 2, slot)
                    if k == 2 and not first:
                        centre1(g - 1, 1 - slot)

            for k in range(XT_STEPS):
                frames_lo(0, k, 0)
            tokens(0, 0, first=True)
            tokens(1, 1, second=True)
            tokens(2, 0)
            with dve.Fori(1, GROUPS // 2 - 1) as j:
                tokens(2 * j + 1, 1)
                tokens(2 * j + 2, 0)
            tokens(GROUPS - 1, 1, last=True)
            inverse1(GROUPS - 2, 0)
            normal1(GROUPS - 2, 0)
            centre1(GROUPS - 1, 1)
            inverse1(GROUPS - 1, 1)
            normal1(GROUPS - 1, 1)

            dve.wait_ge(s_const, 12)
            dve.wait_ge(ln[0]["xn"], GROUPS)

            def wide_heads(v):
                return v.rearrange("p (h a) -> p h a", a=1).to_broadcast([P, HEADS, N])

            def mask(i, s):
                dve.wait_ge(at_s["q"], i + 1)
                for b in range(2):
                    src = ps[:, s, PN:2 * PN].rearrange("p (n b) -> p b n", b=2)[:, b:b + 1, :]
                    op = dve.tensor_tensor(k_blk[:, s, b, :, :], src.to_broadcast([P, HEADS, N]),
                                           wide_heads(head_mask[:, :]), ALU.mult)
                op.then_inc(at_s["k"], 1)
            def shift(i, s):
                sc = ps[:, 2 + s, 0:HEADS * N].rearrange("p (h n) -> p h n", h=HEADS)
                dve.wait_ge(at_s["s"], i + 1)
                dve.reduce_max(smax[:, s, :], sc, AX_X).then_inc(at_s["mx"], 1)
                dve.wait_ge(at_s["mx"], i + 1)
                dve.tensor_tensor(prob[:, s, :, :], sc, wide_heads(smax[:, s, :]), ALU.subtract).then_inc(at_s["sub"], 1)

            def finish(i, s):
                dve.wait_ge(at_s["o"], i + 1)
                dve.reciprocal(o_rec, ps[:, 5, 128:128 + PN]).then_inc(at_s["rec"], 1)
                dve.wait_ge(at_s["rec"], i + 1)
                dve.tensor_tensor(o_st[:, s, :].rearrange("p (n b) -> p b n", b=2),
                                  ps[:, 5, 0:PN].rearrange("p (b n) -> p b n", b=2),
                                  o_rec.rearrange("p (b n) -> p b n", b=2), ALU.mult).then_inc(at_s["ost"], 1)

            def residual(i):
                dve.wait_ge(at_s["pr"], i + 1)
                own = hT[:, bass.ds(i * PN, PN)]
                dve.scalar_tensor_tensor(out=own, in0=ps[:, 6, 0:PN], scalar=bias_cols[:, 1:2], in1=own,
                                         op0=ALU.add, op1=ALU.add).then_inc(at_s["res"], 1)

            def attend(i, q, t=None):
                if runs(t, 4):
                    residual(i - 4)
                if runs(t, 0):
                    mask(i, q % 2)
                if runs(t, 3):
                    finish(i - 3, (q - 3) % 2)
                if runs(t, 1):
                    if t is None or t > 3:
                        dve.wait_ge(at_s["t"], i - 2)
                    shift(i - 1, (q - 1) % 2)

            def norm(g, q):
                if q == 0:
                    dve.wait_ge(ln[1]["xn"], GROUPS + g)
                    dve.wait_ge(ln[1]["mean"], g + 1)
                    dve.tensor_tensor(xc2, hT[:, bass.ds(g * GN, GN)], ps[:, 7, 0:GN], ALU.subtract).then_inc(ln[1]["xc"], 1)
                if q == 3:
                    dve.wait_ge(ln[1]["sd"], GROUPS + g + 1)
                    dve.reciprocal(sq2, sq2).then_inc(ln[1]["rs"], 1)
                    dve.wait_ge(ln[1]["rs"], g + 1)
                    dve.tensor_tensor(xn[:, bass.ds(g * GN, GN)], xc2, sq2, ALU.mult).then_inc(ln[1]["xn"], 1)

            turns(dve, attend, norm)

            def hidden_biases(e, slot):
                dve.tensor_tensor(b1_col[:, 2 * slot:2 * slot + 2, 0], b1T[:, bass.ds(2 * e, 2)], zeros2[:, 0:2],
                                  ALU.add).then_inc(b1_ready, 1)

            count = [0]

            def chain(op):
                count[0] += 1
                op.then_inc(r_s["dve"], 1)

            def chained():
                dve.wait_ge(r_s["dve"], count[0])

            def wide(v):
                return v.rearrange("p (t a) -> p t a", a=1).to_broadcast([P, TILES, E])

            logits = ps[:, 0:3, :].rearrange("p b (t e) -> p (b t) e", e=E)[:, 0:TILES, :]
            dve.wait_ge(r_s["lg"], 1)
            chain(dve.reduce_max(rmax, logits, AX_X))
            chained()
            chain(dve.tensor_tensor(rp, logits, wide(rmax), ALU.subtract))
            dve.wait_ge(r_s["act"], 1)
            chain(dve.reduce_sum(rsum, rp, AX_X))
            chained()
            chain(dve.reciprocal(rinv, rsum))
            chained()
            chain(dve.tensor_scalar(rneg, rinv, -1.0, None, ALU.mult))
            dve.wait_ge(s_b1, 1)
            hidden_biases(0, 0)
            dve.wait_ge(r_s["neg"], 1)
            for rnd in range(ROUNDS):
                for t in range(TILES):
                    op = dve.max(rtop[:, t, :], rs[:, t, :])
                chain(op)
                chained()
                if rnd == ROUNDS - 1:
                    chain(dve.memset(rtop[:, :, LASTDROP:8], TAKEN))
                    chained()
                for t in range(TILES):
                    op = dve.match_replace(rs[:, t, :], rtop[:, t, :], rs[:, t, :], TAKEN)
                chain(op)
                chained()
            dve.wait_ge(r_s["act"], 2)
            chain(dve.scalar_tensor_tensor(out=re, in0=rs[:, :, ::-1], scalar=TAKEN / 2 - 0.5, in1=re,
                                           op0=ALU.is_gt, op1=ALU.mult))
            chained()
            chain(dve.reduce_sum(rsum, re, AX_X))
            chained()
            chain(dve.reciprocal(rsum, rsum))
            chained()
            chain(dve.tensor_tensor(re, re, wide(rsum), ALU.mult))
            assert count[0] == RDVE

            def mul(m, c, gs, cs, loaded):
                s, n = chunks[c]
                if loaded is not None:
                    dve.wait_ge(c_loaded[cs], loaded)
                dve.wait_ge(gelu_done, 2 * m + 2)
                dve.tensor_tensor(gbuf[:, gs, s:s + n], gbuf[:, gs, s:s + n], cbuf[:, cs, s:s + n],
                                  ALU.mult).then_inc(mul_done, 1)

            def low(m, c, gs):
                s, n = chunks[c]
                dve.wait_ge(hi_done, m + 1)
                dve.tensor_tensor(g_lo[:, gs, s:s + n], gbuf[:, gs, s:s + n], g_hi[:, gs, s:s + n].bitcast(F32),
                                  ALU.subtract).then_inc(lo_done, 1)

            def step(n, q, loaded, first, e=None):
                for c in range(NG):
                    if c == 1 and q % 2 == 0 and e is not None:
                        hidden_biases(e + 1, 1 - q // 2)
                    mul(n * NG + c, c, q % 2, q // 2, loaded if c == 0 and q % 2 == 0 else None)
                    if c:
                        low(n * NG + c - 1, c - 1, q % 2)
                    elif not first:
                        low(n * NG - 1, NG - 1, 1 - q % 2)

            for n in range(4):
                step(n, n, 16, n == 0, n // 2)
            with dve.Fori(1, HALVES // 4 - 1) as i:
                for q in range(4):
                    step(4 * i + q, q, 16 * i + 16, False, 2 * i + q // 2)
            for q in range(4):
                n = HALVES - 4 + q
                step(n, q, 16 * (n // 4) + 16, False, n // 2 if q < 2 else None)
            low(HALVES * NG - 1, NG - 1, 1)

            total = ps[:, 0:NB, :].rearrange("p b n -> p (b n)")
            for g in range(GROUPS):
                cols = slice(g * GN, (g + 1) * GN)
                dve.wait_ge(s_acc, (g + 1) * GN // BLK + 1 if g < GROUPS - 1 else NB)
                dve.tensor_tensor(yT[:, cols].rearrange("p (a b n) -> p a b n", a=GP, b=2),
                                  total[:, cols].rearrange("p (a n b) -> p a b n", a=GP, b=2),
                                  hT[:, cols].rearrange("p (a n b) -> p a b n", a=GP, b=2), ALU.add).then_inc(s_y, 1)


RDVE = 5 + 7 + 4


_INS = ["x", "L0_tok_W", "L0_tok_b", "L0_attn_w_qkv", "L0_attn_w_out", "L0_attn_b_out", "L0_ffn_w1", "L0_ffn_b1",
        "L0_ffn_w2", "L0_ffn_b2", "L0_ffn_router_w", "L0_ffn_router_b"]


def kernel(**inputs):
    import numpy as np
    import concourse.bacc as bacc
    from concourse.bass_utils import run_bass_kernel_spmd

    nc = bacc.Bacc("TRN2", target_bir_lowering=False, num_devices=1)
    arrays, args = {}, []
    for name in _INS:
        a = np.ascontiguousarray(inputs[name])
        arrays[f"in_{name}"] = a
        args.append(nc.dram_tensor(f"in_{name}", a.shape, mybir.dt.from_np(a.dtype), kind="ExternalInput").ap())
    clips, frames, width = arrays["in_x"].shape
    patches = -(-(frames - PATCH) // STRIDE) + 1
    y = nc.dram_tensor("out_y", (clips, patches, width), F32, kind="ExternalOutput").ap()
    audio_tower(nc, *args, y)
    r = run_bass_kernel_spmd(nc, [arrays], core_ids=[0])
    return r.results[0]["out_y"]
```

```python
from contextlib import ExitStack

import concourse.bass as bass
from concourse import mybir

ALU = mybir.AluOpType
ACT = mybir.ActivationFunctionType
F32 = mybir.dt.float32
F32R = mybir.dt.float32r
AX_X = mybir.AxisListType.X

P = 128
EPS = 1e-5
PATCH, STRIDE = 16, 8
HEADS = 8
TOPK = 42
TAKEN = -2.0


def audio_tower(nc, x, tok_W, tok_b, w_qkv, w_out, b_out, w1, b1, w2, b2, router_w, router_b, out):
    B, T, D = x.shape
    E, _, H = w1.shape
    N = out.shape[1]
    M = N + 1
    HD = D // HEADS
    SCALE = float(HD) ** -0.5
    PAIRS = B // 2
    PN, PM = 2 * N, 2 * M
    TOK = B * N
    GP = 4
    GROUPS = PAIRS // GP
    GN = GP * PN
    TILES = TOK // P
    RT = -(-GN // P)
    rt_cols = [min(k * P, GN - P) for k in range(RT)]
    assert D == P and TOK % P == 0 and H == 2 * P and E * 2 == P and PATCH == 2 * STRIDE

    BLK = 512
    blocks = [(s, min(BLK, TOK - s)) for s in range(0, TOK, BLK)]
    NB = len(blocks)
    NG = NB // 2
    chunks = [(blocks[2 * c][0], blocks[2 * c][1] + blocks[2 * c + 1][1]) for c in range(NG)]
    HALVES = 2 * E
    DROP = E - TOPK
    ROUNDS = -(-DROP // 8)
    LASTDROP = DROP - 8 * (ROUNDS - 1)

    comb_dram = nc.dram_tensor("comb_scratch", (E, TOK), F32).ap()

    with ExitStack() as ctx:
        def sb(name, shape, dt=F32):
            return ctx.enter_context(nc.sbuf_tensor(name, shape, dt))

        def sem(name):
            return ctx.enter_context(nc.semaphore(name))

        ps = ctx.enter_context(nc.psum_tensor("ps", [P, 8, BLK], F32))

        ident = sb("ident", [P, P])
        ones_mean = sb("ones_mean", [P, P])
        ones_row = sb("ones_row", [1, P])
        centring = sb("centring", [P, P])
        eps_cols = sb("eps_cols", [P, GP])
        ones_sq = sb("ones_sq", [P, P])
        head_mask = sb("head_mask", [P, HEADS])
        parity_mask = sb("parity_mask", [PN, 2, HD])
        W_raw = sb("W_raw", [P, D * PATCH])
        bias_cols = sb("bias_cols", [P, 2])
        wqkv_sb = sb("wqkv_sb", [P, 3 * D])
        wout_sb = sb("wout_sb", [P, D])
        rw_sb = sb("rw_sb", [P, E])
        rb_sb = sb("rb_sb", [1, E])
        b1_raw = sb("b1_raw", [P, P])
        b1T = sb("b1T", [P, HALVES])
        b2_sb = sb("b2_sb", [E, D])
        b1_col = sb("b1_col", [P, 4, 1])
        zeros2 = sb("zeros2", [P, 4])
        pool_tick = sb("pool_tick", [P, 1])

        hT = sb("hT", [P, TOK])

        xn = sb("xn", [P, TOK])[:, :]

        combT_sb = sb("combT_sb", [E, TOK])
        inv = sb("inv", [P, 4, GP])
        minus_half = sb("minus_half", [P, GP])
        dve_tick = sb("dve_tick", [P, 1])
        q_st = sb("q_st", [P, 2, 2, 64])
        x_st = sb("x_st", [P, 2, 2, 2, N])

        gbuf = sb("gbuf", [P, 2, TOK])
        cbuf = sb("cbuf", [P, 2, TOK])
        SLOT = max(TOK, STRIDE * GP * PM)
        parts_hi = sb("parts_hi", [P, 2 * SLOT], F32R)
        parts_lo = sb("parts_lo", [P, 2 * SLOT], F32R)
        g_hi = parts_hi[:, 0:2 * TOK].rearrange("p (s n) -> p s n", s=2)
        g_lo = parts_lo[:, 0:2 * TOK].rearrange("p (s n) -> p s n", s=2)
        x_hi = sb("x_hi", [P, TOK], F32R)
        x_lo = sb("x_lo", [P, TOK], F32R)
        w_raw = sb("w_raw", [P, 2, 2 * H])
        w_hi = sb("w_hi", [P, 2, 2 * H], F32R)
        w_lo = sb("w_lo", [P, 2, 2 * H], F32R)

        gflat = gbuf[:, :, :].rearrange("p a b -> p (a b)")
        cflat = cbuf[:, :, :].rearrange("p a b -> p (a b)")
        xin = gflat[:, 0:GP * STRIDE * D].rearrange("p (a b) -> p a b", a=GP)
        XTN = STRIDE * GP * PM
        xT_hi = parts_hi[:, 0:2 * XTN].rearrange("p (s r a m) -> p s r a m", s=2, r=STRIDE, a=GP)
        xT_lo = parts_lo[:, 0:2 * XTN].rearrange("p (s r a m) -> p s r a m", s=2, r=STRIDE, a=GP)
        WT_hi = x_hi[:, 0:PATCH * P].rearrange("p (f e) -> p f e", f=PATCH)
        WT_lo = x_lo[:, 0:PATCH * P].rearrange("p (f e) -> p f e", f=PATCH)
        xc, sq, diag = (cflat[:, k * GN:(k + 1) * GN] for k in range(3))
        at = [0]

        def carve(cols):
            at[0] += cols
            return cflat[:, at[0] - cols:at[0]]

        k_blk = carve(4 * HEADS * N).rearrange("p (s b h n) -> p s b h n", s=2, b=2, h=HEADS)
        v_blk = carve(8 * D).rearrange("p (s b d) -> p s b d", s=4, b=2)
        prob = carve(4 * HEADS * N).rearrange("p (s h n) -> p s h n", s=4, h=HEADS)
        pT = carve(8 * P).rearrange("p (s c n) -> p s c n", s=2, c=4)
        assert at[0] <= 2 * TOK
        o_st = gflat[:, 0:2 * PN].rearrange("p (s n) -> p s n", s=2)
        smax = gflat[:, 320:320 + 2 * HEADS].rearrange("p (s h) -> p s h", s=2)
        ssum = gflat[:, 352:352 + 2 * HEADS].rearrange("p (s h) -> p s h", s=2)
        xc2, sq2, diag2 = (gflat[:, TOK + k * GN:TOK + (k + 1) * GN] for k in range(3))
        xg = gflat[:, TOK + 3 * GN:TOK + 4 * GN]
        xc3, sq3, diag3, xg3 = (gflat[:, TOK + k * GN:TOK + (k + 1) * GN] for k in range(4, 8))
        BANK3 = 1
        GW = RT * E
        comb = W_raw[:, 0:GROUPS * GW]
        rflat = sb("rflat", [P, 3 * GW + 12 * RT])
        rp, rs, re = (rflat[:, k * GW:(k + 1) * GW].rearrange("p (t e) -> p t e", e=E) for k in range(3))
        rw = 3 * GW
        rtop = rflat[:, rw:rw + 8 * RT].rearrange("p (t k) -> p t k", k=8)
        rmax, rinv, rneg, rsum = (rflat[:, rw + (8 + k) * RT:rw + (9 + k) * RT] for k in range(4))
        combT = combT_sb[:, :]
        yT = gflat[:, 0:TOK]
        y_st = cflat[:, 0:TOK].rearrange("p (t d) -> p t d", d=D)

        s_const = sem("s_const")
        s_bias = sem("s_bias")
        s_small = sem("s_small")
        s_wraw = sem("s_wraw")
        s_wt = sem("s_wt")
        s_wt_hi = sem("s_wt_hi")
        s_wt_lo = sem("s_wt_lo")
        s_xzero = sem("s_xzero")
        s_xin = [sem(f"s_xin{p}") for p in range(GP)]
        s_xt = sem("s_xt")
        s_xt_hi = sem("s_xt_hi")
        s_xt_lo = sem("s_xt_lo")
        s_tok = sem("s_tok")
        s_tok_out = sem("s_tok_out")
        ln = {k: sem(f"s_ln_{k}") for k in ("xc", "sq", "var", "ve", "inv", "diag", "wide", "xn")}
        at_s = {k: sem(f"s_at_{k}") for k in ("xst", "qk", "q", "k", "s", "mx", "sub", "exp", "sum", "rec", "p", "t", "pt", "o",
                                              "ost", "pr", "res", "zero")}
        r_s = {k: sem(f"s_r_{k}") for k in ("xh", "xl", "lg", "dve", "sub", "act", "neg", "inv", "ex", "cw", "t", "ct", "b2")}
        s_dram = [sem(f"s_dram{c}") for c in range(3)]
        s_b1t = sem("s_b1t")
        s_b1 = sem("s_b1")
        w_loaded = [sem(f"w_loaded{s}") for s in range(2)]
        c_loaded = [sem(f"c_loaded{s}") for s in range(2)]
        c_first = [[sem(f"c_first{e}{c}") for c in range(3)] for e in range(2)]
        s_acc = sem("s_acc")
        w_split = sem("w_split")
        s_tick = sem("s_tick")
        s_centring = sem("s_centring")
        b1_ready = sem("b1_ready")
        w_hi_done = sem("w_hi_done")
        up_done = sem("up_done")
        gelu_done = sem("gelu_done")
        mul_done = sem("mul_done")
        hi_done = sem("hi_done")
        lo_done = sem("lo_done")
        down_done = sem("down_done")
        s_y = sem("s_y")
        s_yt = sem("s_yt")
        s_yst = sem("s_yst")
        s_out = sem("s_out")

        LAG = 5

        def runs(t, lag):
            return t is None or lag <= t < PAIRS + lag

        def is_last_but_one(g):
            return isinstance(g, int) and g == GROUPS - 2

        def turns(eng, attend, norm, route, finish=lambda i, q, t=None: None):
            for t in range(3 * GP):
                attend(t, t % 4, t)
                if t >= 2 * GP:
                    norm(0, GROUPS, t % 4)
                finish(t, t % 4, t)
            with eng.Fori(3, GROUPS) as j:
                for q in range(4):
                    attend(4 * j + q, q)
                    norm(j - 2, GROUPS + j - 2, q)
                    route(j - 3, q)
                    finish(4 * j + q, q)
            for t in range(PAIRS, PAIRS + LAG):
                attend(t, t % 4, t)
                if t < PAIRS + GP:
                    norm(GROUPS - 2, 2 * GROUPS - 2, t % 4)
                    route(GROUPS - 3, t % 4)
                finish(t, t % 4, t)

        COMBINED = {PAIRS + 1: (0,), PAIRS + 2: (1, 2)}
        COMB_BANK = (0, 2, 3, 4, 5, 0, 2, 3)
        LAST_COMBINED = (0, 1)

        block = ctx.enter_context(nc.Block())

        OUT_TILES = [(t, min(t + 4, TILES)) for t in range(0, TILES, 4)]
        XT_STEPS = 2 * GP
        EX2 = E // 2 - 1

        @block.sync
        def _(sp):
            nc_ = sp
            nc_.dma_start(W_raw[:, :], tok_W).then_inc(s_wraw, 16)
            sp.wait_ge(s_xzero, 1)

            SPLIT = 32

            def frames(g, p):
                pair = g * GP + p
                rows = x[bass.ds(2 * pair, 2), 0:N * STRIDE, :].rearrange("b (m r) d -> m b (r d)", r=STRIDE)
                sp.dma_start(xin[0:2 * SPLIT, p, :], rows[0:SPLIT, :, :]).then_inc(s_xin[p], 16)
                sp.dma_start(xin[2 * SPLIT:PN, p, :], rows[SPLIT:N, :, :]).then_inc(s_xin[p], 16)
                rest = x[bass.ds(2 * pair, 2), N * STRIDE:T, :].rearrange("b r d -> b (r d)")
                sp.dma_start(xin[PN:PM, p, 0:(T - N * STRIDE) * D], rest).then_inc(s_xin[p], 16)

            for p in range(GP):
                frames(0, p)
            small = [(bias_cols[:, 0:1], tok_b.rearrange("(p a) -> p a", a=1)),
                     (bias_cols[:, 1:2], b_out.rearrange("(p a) -> p a", a=1)),
                     (wqkv_sb[:, :], w_qkv), (wout_sb[:, :], w_out), (rw_sb[:, :], router_w),
                     (rb_sb[:, :], router_b.rearrange("(a e) -> a e", a=1)),
                     (b1_raw[:, :], b1.rearrange("e (j h) -> (e j) h", j=2)), (b2_sb[:, :], b2)]
            for dst, src in small:
                sp.dma_start(dst, src).then_inc(s_small, 16)
            def weights(e, slot):
                sp.dma_start(w_raw[:, slot, 0:H], w1[bass.ds(e, 1), :, :].rearrange("a d h -> d (a h)")).then_inc(w_loaded[slot], 16)
                sp.dma_start(w_raw[:, slot, H:2 * H].rearrange("p (j d) -> p j d", j=2),
                             w2[bass.ds(e, 1), :, :].rearrange("a (j p) d -> p (a j) d", j=2)).then_inc(w_loaded[slot], 16)

            for e in range(2):
                weights(e, e)
            with sp.Fori(1, GROUPS) as g:
                for p in range(GP):
                    sp.wait_ge(s_xt, (g - 1) * XT_STEPS + 2 * p + 2)
                    frames(g, p)

            def combine(e, slot):
                sp.dma_start(cbuf[:, slot, :], comb_dram[bass.ds(e, 1), :].to_broadcast([P, TOK])).then_inc(c_loaded[slot], 16)

            for c, (s, n) in enumerate(chunks):
                sp.wait_ge(r_s["ct"], -(-(s + n) // GN))
                if c == 0:
                    sp.wait_ge(at_s["res"], PAIRS)
                sp.dma_start(comb_dram[:, s:s + n], combT[:, s:s + n]).then_inc(s_dram[c], 16)
                sp.wait_ge(s_dram[c], 16)
                for e in range(2):
                    sp.dma_start(cbuf[:, e, s:s + n], comb_dram[e:e + 1, s:s + n].to_broadcast([P, n])).then_inc(c_first[e][c], 16)
            with sp.Fori(0, EX2) as i:
                for slot in range(2):
                    sp.wait_ge(w_split, 2 * i + slot + 1)
                    weights(2 * i + 2 + slot, slot)
                    sp.wait_ge(mul_done, (2 * i + slot + 1) * 2 * NG)
                    combine(2 * i + 2 + slot, slot)

            rows = out.rearrange("b n d -> (b n) d").rearrange("(t p) d -> p t d", p=P)
            for c, (t0, t1) in enumerate(OUT_TILES):
                sp.wait_ge(s_yst, c + 1)
                sp.dma_start(rows[:, t0:t1, :], y_st[:, t0:t1, :]).then_inc(s_out, 16)
            sp.wait_ge(s_out, 16 * len(OUT_TILES))

        @block.gpsimd
        def _(pool):
            pool.memset(gflat[:, 0:GP * STRIDE * D], 0.0).then_inc(s_xzero, 1)
            pool.memset(pool_tick[:, :], 0.0).then_inc(s_tick, 1)
            pool.memset(ident[:, :], 0.0).then_inc(s_const, 1)
            pool.memset(ones_mean[:, :], 1.0 / D).then_inc(s_const, 1)
            pool.memset(ones_row[:, :], 1.0).then_inc(s_const, 1)
            pool.memset(eps_cols[:, :], EPS).then_inc(s_const, 1)
            pool.memset(minus_half[:, :], -0.5).then_inc(s_const, 1)
            pool.memset(ones_sq[:, :], 1.0).then_inc(s_const, 1)
            pool.memset(head_mask[:, :], 1.0).then_inc(s_const, 1)
            pool.memset(parity_mask[:, :, :], 1.0).then_inc(s_const, 1)
            pool.memset(zeros2[:, :], 0.0).then_inc(s_const, 1)
            pool.wait_ge(s_const, 9)
            pool.affine_select(out=ident[:, :], in_=ident[:, :], compare_op=ALU.not_equal, fill=1.0, base=0,
                               pattern=[[-1, P]], channel_multiplier=1).then_inc(s_const, 1)
            pool.affine_select(out=head_mask[:, :], in_=head_mask[:, :], compare_op=ALU.is_ge, fill=0.0, base=0,
                               pattern=[[-HD, HEADS]], channel_multiplier=1).then_inc(s_const, 1)
            pool.affine_select(out=parity_mask[:, 0, :], in_=parity_mask[:, 0, :], compare_op=ALU.is_ge, fill=0.0,
                               base=N - 1, pattern=[[0, HD]], channel_multiplier=-1).then_inc(s_const, 1)
            pool.affine_select(out=parity_mask[:, 1, :], in_=parity_mask[:, 1, :], compare_op=ALU.is_ge, fill=0.0,
                               base=-N, pattern=[[0, HD]], channel_multiplier=1).then_inc(s_const, 1)
            pool.wait_ge(s_const, 13)
            pool.affine_select(out=head_mask[:, :], in_=head_mask[:, :], compare_op=ALU.is_ge, fill=0.0, base=HD - 1,
                               pattern=[[HD, HEADS]], channel_multiplier=-1).then_inc(s_const, 1)
            pool.wait_ge(s_const, 14)

            def invert(n, a, dg):
                pool.wait_ge(ln["ve"], n + 1)
                pool.tensor_tensor(inv[0:PN, a + 1, :], inv[0:PN, a, :], minus_half[0:PN, :], ALU.pow).then_inc(ln["inv"], 1)
                pool.wait_ge(ln["inv"], n + 1)
                pool.tensor_tensor(dg[0:PN, :].rearrange("p (a n) -> p a n", a=GP),
                                   ident[0:PN, 0:PN].rearrange("p (a n) -> p a n", a=1).to_broadcast([PN, GP, PN]),
                                   inv[0:PN, a + 1, :].rearrange("p (a n) -> p a n", n=1).to_broadcast([PN, GP, PN]),
                                   ALU.mult).then_inc(ln["diag"], 1)

            pool.memset(q_st[:, :, :, :], 0.0).then_inc(at_s["zero"], 1)

            def split(e, slot, use):
                first = isinstance(use, int)
                pool.wait_ge(w_loaded[slot], 32 * (use + 1))
                if not first:
                    pool.wait_ge(s_tick, e - 1)
                    pool.wait_ge(down_done, (e - 1) * 2 * NG)
                    pool.tensor_tensor(pool_tick[:, :], eps_cols[:, 0:1], eps_cols[:, 0:1], ALU.add).then_inc(s_tick, 1)
                pool.tensor_copy(w_hi[:, slot, :], w_raw[:, slot, :]).then_inc(w_hi_done, 1)
                pool.wait_ge(w_hi_done, e + 1)
                pool.tensor_tensor(w_lo[:, slot, :], w_raw[:, slot, :], w_hi[:, slot, :].bitcast(F32),
                                   ALU.subtract).then_inc(w_split, 1)

            for e in range(2):
                split(e, e, 0)

            with pool.Fori(0, GROUPS - 1) as g:
                invert(g, 0, diag)

            def stage(i, s):
                src = xn[:, bass.ds(i * PN, PN)].rearrange("p (n b) -> p b n", b=2)
                for c in range(2):
                    pool.tensor_copy(x_st[:, s, :, c, :], src).then_inc(at_s["xst"], 1)

            pool.wait_ge(ln["xn"], 1)
            for i in range(2):
                stage(i, i)
            invert(GROUPS - 1, 0, diag)
            pool.wait_ge(ln["xn"], GROUPS)

            def attend(i, q, t=None):
                if runs(t, 0) and (t is None or t >= 2):
                    pool.wait_ge(at_s["qk"], i - 1)
                    stage(i, q % 2)
                if runs(t, 3):
                    pool.wait_ge(at_s["rec"], i - 2)
                    s = (q - 3) % 4
                    pool.tensor_tensor(prob[:, s, :, :], prob[:, s, :, :],
                                       ssum[:, s % 2, :].rearrange("p (h a) -> p h a", a=1).to_broadcast([P, HEADS, N]),
                                       ALU.mult).then_inc(at_s["p"], 1)

            def norm(g, n, q):
                if q == 3:
                    invert(n, 0, diag2)

            def route(g, q, tokens=xg):
                if q == 1:
                    pool.wait_ge(r_s["xh"], g + 1)
                    cols = bass.ds(g * GN, GN)
                    pool.tensor_tensor(x_lo[:, cols], tokens, x_hi[:, cols].bitcast(F32), ALU.subtract).then_inc(r_s["xl"], 1)

            turns(pool, attend, norm, route)
            invert(2 * GROUPS - 1, 2, diag3)
            route(GROUPS - 2, 1)
            route(GROUPS - 1, 1, xg3)

            with pool.Fori(0, EX2) as i:
                for slot in range(2):
                    split(2 * i + 2 + slot, slot, i + 1)

        @block.tensor
        def _(pe):
            pe.wait_ge(s_const, 14)
            pe.wait_ge(s_wraw, 16)
            Wv = W_raw[:, :].rearrange("e (d f) -> e f d", f=PATCH)
            for f in range(PATCH):
                mm = pe.transpose(ps[:, 4 + f // 4, f % 4 * P:(f % 4 + 1) * P], Wv[:, f, :], ident[:, :])
                if f % 4 == 3:
                    mm.then_inc(s_wt, 1)

            def transpose_frames(g, k, first):
                p, half = k // 2, k % 2
                if half == 0:
                    pe.wait_ge(s_xin[p], 48 * (g + 1))
                if not (first and k < 4):
                    pe.wait_ge(s_xt_lo, g * XT_STEPS + k - 3)
                for c in range(4):
                    r = 4 * half + c
                    mm = pe.transpose(ps[:, k % 4, c * PM:(c + 1) * PM], xin[0:PM, p, r * D:(r + 1) * D],
                                      ident[0:PM, 0:PM])
                mm.then_inc(s_xt, 1)

            def embed(g, f, slot):
                r, s = f % STRIDE, f // STRIDE
                hi = xT_hi[:, slot, r, :, 2 * s:2 * s + PN]
                lo = xT_lo[:, slot, r, :, 2 * s:2 * s + PN]
                o = ps[:, 4 + slot, 0:GN]
                pe.matmul(o, WT_hi[:, f, :], lo, start=(f == 0), stop=False)
                pe.matmul(o, WT_lo[:, f, :], hi, start=False, stop=False)
                mm = pe.matmul(o, WT_hi[:, f, :], hi, start=False, stop=(f == PATCH - 1))
                if f == PATCH - 1:
                    mm.then_inc(s_tok, 1)

            def centre(g, n, bank=7):
                if bank == 7 and not (isinstance(n, int) and n == 0):
                    pe.wait_ge(ln["xn"], n)
                pe.matmul(ps[:, bank, 0:GN], centring[:, :], hT[:, bass.ds(g * GN, GN)],
                          start=True, stop=True).then_inc(ln["xc"], 1)

            def variance(n, squares, bank=7):
                pe.wait_ge(ln["sq"], n + 1)
                for a in range(GP):
                    mm = pe.matmul(ps[0:PN, bank, GN + 2 * a:GN + 2 * a + 1], squares[:, a * PN:(a + 1) * PN], ones_mean[:, 0:1],
                                   start=True, stop=True)
                mm.then_inc(ln["var"], 1)

            def spread(n, dg, bank=7):
                pe.wait_ge(ln["diag"], n + 1)
                pe.matmul(ps[:, bank, 0:GN], ones_sq[0:PN, :], dg[0:PN, :], start=True, stop=True).then_inc(ln["wide"], 1)

            def tokens(g, slot, last=False, first=False):
                pe.wait_ge(s_xt_lo, (g + 1) * XT_STEPS)
                for k in range(XT_STEPS):
                    if not last:
                        transpose_frames(g + 1, k, False)
                    for f in range(2 * k, 2 * k + 2):
                        embed(g, f, slot)
                    if k == 0 and not first:
                        pe.wait_ge(s_tok_out, g)
                        centre(g - 1, g - 1)
                    if k == 3 and not first:
                        variance(g - 1, sq)
                    if k == 6 and not first:
                        spread(g - 1, diag)

            for k in range(XT_STEPS):
                transpose_frames(0, k, True)
            pe.wait_ge(s_wt_lo, 4)
            pe.wait_ge(s_centring, 1)
            tokens(0, 0, first=True)
            tokens(1, 1)
            tokens(2, 0)
            with pe.Fori(1, GROUPS // 2 - 1) as j:
                tokens(2 * j + 1, 1)
                tokens(2 * j + 2, 0)
            tokens(GROUPS - 1, 1, last=True)
            pe.wait_ge(s_small, 16 * 8)

            def project_in(i, s, first):
                tok = xn[:, bass.ds(i * PN, PN)]
                if not first:
                    pe.wait_ge(at_s["k"], i - 1)
                pe.matmul(ps[:, s, 0:PN], wqkv_sb[:, 0:D], tok, start=True, stop=True)
                pe.matmul(ps[:, s, PN:2 * PN], wqkv_sb[:, D:2 * D], tok, start=True, stop=True)
                pe.wait_ge(at_s["xst"], 2 * i + 2)
                for b in range(2):
                    mm = pe.matmul(ps[0:PN, s, 2 * PN + b * D:2 * PN + (b + 1) * D], x_st[:, s, b, :, :],
                                   wqkv_sb[:, 2 * D:3 * D], start=True, stop=True)
                mm.then_inc(at_s["qk"], 1)

            pe.wait_ge(s_tok_out, GROUPS)
            centre(GROUPS - 1, GROUPS - 1)
            pe.transpose(ps[:, 6, 0:P], b1_raw[:, :], ident[:, :]).then_inc(s_b1t, 1)
            project_in(0, 0, True)
            variance(GROUPS - 1, sq)
            project_in(1, 1, True)
            spread(GROUPS - 1, diag)
            pe.wait_ge(ln["xn"], GROUPS)

            def scores(i, s, first):
                pe.wait_ge(at_s["k"], i + 1)
                if not first:
                    pe.wait_ge(at_s["sub"], i - 1)
                for b in range(2):
                    mm = pe.matmul(ps[64 * b:64 * b + 64, 2 + s, 0:HEADS * N], q_st[:, s, b, :], k_blk[:, s, b, :, :],
                                   start=True, stop=True)
                mm.then_inc(at_s["s"], 1)

            def flip(i, s4, first):
                pe.wait_ge(at_s["p"], i + 1)
                if not first:
                    pe.wait_ge(at_s["pt"], i)
                for c in range(4):
                    mm = pe.transpose(ps[0:PN, 4, c * P:(c + 1) * P], prob[:, s4, 2 * c:2 * c + 2, :], ident[:, :])
                mm.then_inc(at_s["t"], 1)

            def weigh(i, s, vs, first):
                pe.wait_ge(at_s["pt"], i + 1)
                if not first:
                    pe.wait_ge(at_s["ost"], i)
                for c in range(4):
                    for b in range(2):
                        rows = slice(32 * c, 32 * c + 32)
                        mm = pe.matmul(ps[rows, 5, b * N:(b + 1) * N], v_blk[0:PN, vs, b, rows],
                                       pT[0:PN, s, c, 64 * b:64 * b + N], start=True, stop=True)
                mm.then_inc(at_s["o"], 1)

            def project_out(i, s, first):
                pe.wait_ge(at_s["ost"], i + 1)
                if first:
                    pe.wait_ge(s_b1, 1)
                else:
                    pe.wait_ge(at_s["res"], i)
                pe.matmul(ps[:, 6, 0:PN], wout_sb[:, :], o_st[:, s, :], start=True, stop=True).then_inc(at_s["pr"], 1)

            def attend(i, q, t=None):
                if runs(t, 4):
                    weigh(i - 4, q % 2, q % 4, t == 4)
                if runs(t, 0) and (t is None or t >= 2):
                    project_in(i, q % 2, False)
                if runs(t, 1):
                    scores(i - 1, (q - 1) % 2, t in (1, 2))
                if runs(t, 3):
                    flip(i - 3, (q - 3) % 4, t == 3)
                if runs(t, 5):
                    project_out(i - 5, (q - 5) % 2, t == 5)

            def norm(g, n, q):
                if q == 1:
                    pe.wait_ge(at_s["res"], GP * (g + 1))
                    if not (isinstance(g, int) and g == 0):
                        pe.wait_ge(r_s["sub"], g)
                    centre(g, n)
                if q == 2:
                    variance(n, sq2)
                if q == 3 and not is_last_but_one(g):
                    spread(n, diag2)

            def route(g, q, tokens=xg, bank=7):
                if q == 0:
                    pe.wait_ge(ln["xn"], GROUPS + g + 1)
                    pe.matmul(ps[:, bank, 0:RT * E], ones_row[:, :], rb_sb[:, :].rearrange("p (a e) -> p a e", a=1)
                              .to_broadcast([1, RT, E]), start=True, stop=False, skip_group_check=True)
                    for k, at_col in enumerate(rt_cols):
                        mm = pe.matmul(ps[:, bank, k * E:(k + 1) * E], tokens[:, at_col:at_col + P], rw_sb[:, :],
                                       start=False, stop=(k == RT - 1), skip_group_check=True)
                    mm.then_inc(r_s["lg"], 1)

            def combine(g, bank):
                pe.wait_ge(r_s["cw"], g + 1)
                for k, at_col in enumerate(rt_cols):
                    mm = pe.transpose(ps[0:E, bank, at_col:at_col + P], comb[:, (g * RT + k) * E:(g * RT + k + 1) * E],
                                      ident[:, :])
                mm.then_inc(r_s["t"], 1)

            def finish(i, q, t=None):
                if t == PAIRS + 1:
                    pe.wait_ge(at_s["k"], PAIRS)
                if t == PAIRS + 2:
                    pe.wait_ge(at_s["sub"], PAIRS)
                for g in COMBINED.get(t, ()):
                    combine(g, COMB_BANK[g])

            turns(pe, attend, norm, route, finish)
            spread(2 * GROUPS - 2, diag2)
            pe.wait_ge(at_s["res"], PAIRS)
            centre(GROUPS - 1, 2 * GROUPS - 1, BANK3)
            combine(3, COMB_BANK[3])
            route(GROUPS - 2, 0)
            variance(2 * GROUPS - 1, sq3, BANK3)
            combine(4, COMB_BANK[4])
            pe.wait_ge(r_s["ct"], 1)
            combine(5, COMB_BANK[5])
            spread(2 * GROUPS - 1, diag3, BANK3)
            route(GROUPS - 1, 0, xg3, BANK3)

            def up(k0, t, w, free):
                s, n = blocks[t]
                slot, j = w
                if free:
                    pe.wait_ge(gelu_done, k0 + t - 1)
                cols = slice(j * P, (j + 1) * P)
                o = ps[:, 6 + t % 2, 0:n]
                pe.matmul(o, w_hi[:, slot, cols], x_lo[:, s:s + n], start=True, stop=False)
                pe.matmul(o, w_lo[:, slot, cols], x_hi[:, s:s + n], start=False, stop=False)
                pe.matmul(o, w_hi[:, slot, cols], x_hi[:, s:s + n], start=False, stop=True).then_inc(up_done, 1)

            def down(m0, t, w, gs, last=False):
                s, n = blocks[t]
                slot, j = w
                if t % 2 == 0:
                    pe.wait_ge(lo_done, m0 + t // 2 + 1)
                cols = slice(H + j * P, H + (j + 1) * P)
                o = ps[:, t, 0:n]
                pe.matmul(o, w_hi[:, slot, cols], g_lo[:, gs, s:s + n], start=False, stop=False, skip_group_check=True)
                pe.matmul(o, w_lo[:, slot, cols], g_hi[:, gs, s:s + n], start=False, stop=False, skip_group_check=True)
                mm = pe.matmul(o, w_hi[:, slot, cols], g_hi[:, gs, s:s + n], start=False, stop=last, skip_group_check=True)
                if last:
                    mm.then_inc(s_acc, 1)
                elif t % 2 == 1:
                    mm.then_inc(down_done, 1)

            def step(n, q):
                for t in range(NB):
                    if t == 0 and q % 2 == 0:
                        pe.wait_ge(w_split, (n + 2) // 2 if isinstance(n, int) else n[1])
                    nn = n if isinstance(n, int) else n[0]
                    up(nn * NB, t, (q // 2, q % 2), True)
                    pq = (q - 1) % 4
                    down((nn - 1) * NG, t, (pq // 2, pq % 2), pq % 2)

            pe.wait_ge(w_split, 1)
            pe.wait_ge(r_s["sub"], GROUPS - 1)
            pe.wait_ge(r_s["xl"], GROUPS)
            pe.wait_ge(r_s["ct"], 3)
            combine(GROUPS - 2, COMB_BANK[GROUPS - 2])
            for j in range(2):
                for t in range(NB):
                    up(j * NB, t, (0, j), j or t >= 2)
                    if (j, t) == LAST_COMBINED:
                        combine(GROUPS - 1, COMB_BANK[GROUPS - 1])
            pe.wait_ge(r_s["ct"], GROUPS)
            for t, (s, n) in enumerate(blocks):
                mm = pe.matmul(ps[:, t, 0:n], b2_sb[:, :], combT[:, s:s + n], start=True, stop=False, skip_group_check=True)
            mm.then_inc(r_s["b2"], 1)
            for t in range(NB):
                down(0, t, (0, 0), 0)
            for n in range(2, 5):
                step(n, n % 4)
            with pe.Fori(1, EX2) as i:
                for q in range(4):
                    step((4 * i + 1 + q, 2 * i + (q + 3) // 2), (1 + q) % 4)
            for n in range(4 * EX2 + 1, HALVES):
                step(n, n % 4)
            for t in range(NB):
                down((HALVES - 1) * NG, t, (1, 1), 1, last=True)
            for c, (t0, t1) in enumerate(OUT_TILES):
                pe.wait_ge(s_y, -(-t1 * P // GN))
                if c >= 2:
                    pe.wait_ge(s_yst, c - 1)
                for t in range(t0, t1):
                    mm = pe.transpose(ps[:, 6 + c % 2, (t - t0) * P:(t - t0 + 1) * P], yT[:, t * P:(t + 1) * P], ident[:, :])
                mm.then_inc(s_yt, 1)

        @block.scalar
        def _(act):
            for c in range(4):
                act.wait_ge(s_wt, c + 1)
                act.activation(WT_hi[:, 4 * c:4 * c + 4, :], ps[:, 4 + c, :].rearrange("p (f e) -> p f e", f=4),
                               ACT.Copy).then_inc(s_wt_hi, 1)

            def frames_hi(g, k, slot):
                act.wait_ge(s_xt, g * XT_STEPS + k + 1)
                p, half = k // 2, k % 2
                act.activation(xT_hi[:, slot, 4 * half:4 * half + 4, p, :],
                               ps[:, k % 4, 0:4 * PM].rearrange("p (r m) -> p r m", r=4), ACT.Copy).then_inc(s_xt_hi, 1)

            def tokens_out(g, slot):
                act.wait_ge(s_tok, g + 1)
                act.activation(hT[:, bass.ds(g * GN, GN)], ps[:, 4 + slot, 0:GN], ACT.Identity,
                               bias=bias_cols[:, 0:1]).then_inc(s_tok_out, 1)

            def square(n, c, squares, bank=7):
                act.wait_ge(ln["xc"], n + 1)
                act.activation(c, ps[:, bank, 0:GN], ACT.Copy)
                act.activation(squares, ps[:, bank, 0:GN], ACT.Square).then_inc(ln["sq"], 1)

            def tokens(g, slot, last=False, first=False):
                if not first:
                    tokens_out(g - 1, 1 - slot)
                for k in range(XT_STEPS):
                    if not last:
                        frames_hi(g + 1, k, 1 - slot)
                    if k == 2 and not first:
                        square(g - 1, xc, sq)

            for k in range(XT_STEPS):
                frames_hi(0, k, 0)
            act.wait_ge(s_small, 16 * 8)
            tokens(0, 0, first=True)
            with act.Fori(0, GROUPS // 2 - 1) as j:
                tokens(2 * j + 1, 1)
                tokens(2 * j + 2, 0)
            tokens(GROUPS - 1, 1, last=True)
            tokens_out(GROUPS - 1, 1)
            square(GROUPS - 1, xc, sq)
            act.wait_ge(s_b1t, 1)
            act.activation(b1T[:, :], ps[:, 6, 0:P], ACT.Copy).then_inc(s_b1, 1)

            act.wait_ge(at_s["zero"], 1)

            def attend(i, q, t=None):
                if runs(t, 0):
                    act.wait_ge(at_s["qk"], i + 1)
                    s = q % 2
                    act.activation(q_st[:, s, :, 0:N], ps[:, s, 0:PN].rearrange("p (n b) -> p b n", b=2),
                                   ACT.Copy, scale=SCALE)
                    src = ps[0:PN, s, 2 * PN:2 * PN + 2 * D].rearrange("p (c u d) -> p c u d", u=2, d=HD)
                    dst = v_blk[0:PN, q, :, :].rearrange("p b (c u d) -> p (b c) u d", u=2, d=HD)
                    for u in range(2):
                        op = act.activation(dst[:, :, u, :], src[:, :, u, :], ACT.Copy, scale=parity_mask[0:PN, u, 0:1])
                    op.then_inc(at_s["q"], 1)
                if runs(t, 2):
                    act.wait_ge(at_s["sub"], i - 1)
                    s = (q - 2) % 4
                    act.activation(prob[:, s, :, :], prob[:, s, :, :], ACT.Exp).then_inc(at_s["exp"], 1)

            def combine(g, bank):
                act.wait_ge(r_s["t"], g + 1)
                act.activation(combT[:, g * GN:(g + 1) * GN], ps[0:E, bank, 0:GN], ACT.Copy).then_inc(r_s["ct"], 1)

            def finish(i, q, t=None):
                if runs(t, 4):
                    act.wait_ge(at_s["o"], i - 3)
                    act.activation(o_st[:, q % 2, :].rearrange("p (n b) -> p b n", b=2),
                                   ps[:, 5, 0:PN].rearrange("p (b n) -> p b n", b=2), ACT.Copy).then_inc(at_s["ost"], 1)
                if runs(t, 3):
                    act.wait_ge(at_s["t"], i - 2)
                    act.activation(pT[0:PN, (q - 3) % 2, :, :], ps[0:PN, 4, :].rearrange("p (c n) -> p c n", c=4),
                                   ACT.Copy).then_inc(at_s["pt"], 1)
                for g in COMBINED.get(t, ()):
                    combine(g, COMB_BANK[g])

            def norm(g, n, q):
                if q == 2:
                    square(n, xc2, sq2)

            def route(g, q, tokens=xg):
                if q == 1:
                    act.wait_ge(r_s["sub"], g + 1)
                    act.activation(rp, rp, ACT.Exp).then_inc(r_s["act"], 1)
                    act.wait_ge(r_s["act"], g + 1)
                    act.activation(rs[:, :, ::-1], rp, ACT.Copy, scale=-1.0).then_inc(r_s["neg"], 1)
                    act.activation(x_hi[:, bass.ds(g * GN, GN)], tokens, ACT.Copy).then_inc(r_s["xh"], 1)
                if q == 3:
                    act.wait_ge(r_s["inv"], g + 1)
                    for k in range(RT):
                        op = act.activation(re[:, k, :], rp[:, k, :], ACT.Exp, scale=rinv[:, k:k + 1], bias=rneg[:, k:k + 1])
                    op.then_inc(r_s["ex"], 1)

            turns(act, attend, norm, route, finish)
            square(2 * GROUPS - 1, xc3, sq3, BANK3)
            combine(3, COMB_BANK[3])
            route(GROUPS - 2, 1)
            combine(4, COMB_BANK[4])
            route(GROUPS - 2, 3)
            combine(5, COMB_BANK[5])
            route(GROUPS - 1, 1, xg3)
            route(GROUPS - 1, 3)

            def gelu(n, t, gs, b):
                s, m = blocks[t]
                act.wait_ge(up_done, n * NB + t + 1)
                act.activation(gbuf[:, gs, s:s + m], ps[:, 6 + t % 2, 0:m], ACT.Gelu,
                               bias=b1_col[:, b, :]).then_inc(gelu_done, 1)

            def high(m, c, gs, free):
                s, n = chunks[c]
                act.wait_ge(mul_done, m + 1)
                if free:
                    act.wait_ge(down_done, m + 1 - 2 * NG)
                act.activation(g_hi[:, gs, s:s + n], gbuf[:, gs, s:s + n], ACT.Copy).then_inc(hi_done, 1)

            def step(n, gs, first, early, q=None):
                b = n if q is None else q
                if b % 2 == 0:
                    act.wait_ge(b1_ready, n // 2 + 1 if q is None else 2 * i + q // 2 + 1)
                for c in range(NG):
                    if not early:
                        act.wait_ge(lo_done, (n - 2) * NG + c + 1)
                    gelu(n, 2 * c, gs, b)
                    gelu(n, 2 * c + 1, gs, b)
                    if c == 0:
                        if not first:
                            high(n * NG - 1, NG - 1, 1 - gs, b >= 3 or q is not None)
                    else:
                        high(n * NG + c - 1, c - 1, gs, not early)

            act.wait_ge(b1_ready, 1)
            combine(GROUPS - 2, COMB_BANK[GROUPS - 2])
            for n in range(2):
                for t in range(NB):
                    gelu(n, t, n, n)
                    if (n, t) == LAST_COMBINED:
                        combine(GROUPS - 1, COMB_BANK[GROUPS - 1])
            for c in range(NG):
                high(c, c, 0, False)
            for c in range(NG - 1):
                high(NG + c, c, 1, False)
            step(2, 0, False, False)
            step(3, 1, False, False)
            with act.Fori(1, HALVES // 4) as i:
                for q in range(4):
                    step(4 * i + q, q % 2, False, False, q)
            high(HALVES * NG - 1, NG - 1, 1, True)
            for c, (t0, t1) in enumerate(OUT_TILES):
                act.wait_ge(s_yt, c + 1)
                act.activation(y_st[:, t0:t1, :], ps[:, 6 + c % 2, 0:(t1 - t0) * P].rearrange("p (t d) -> p t d", d=D),
                               ACT.Copy).then_inc(s_yst, 1)

        @block.vector
        def _(dve):
            for c in range(4):
                dve.wait_ge(s_wt_hi, c + 1)
                dve.tensor_tensor(WT_lo[:, 4 * c:4 * c + 4, :], ps[:, 4 + c, :].rearrange("p (f e) -> p f e", f=4),
                                  WT_hi[:, 4 * c:4 * c + 4, :].bitcast(F32), ALU.subtract).then_inc(s_wt_lo, 1)

            def frames_lo(g, k, slot):
                dve.wait_ge(s_xt_hi, g * XT_STEPS + k + 1)
                p, half = k // 2, k % 2
                rows = slice(4 * half, 4 * half + 4)
                dve.tensor_tensor(xT_lo[:, slot, rows, p, :], ps[:, k % 4, 0:4 * PM].rearrange("p (r m) -> p r m", r=4),
                                  xT_hi[:, slot, rows, p, :].bitcast(F32), ALU.subtract).then_inc(s_xt_lo, 1)

            def plus_eps(n, a=0, bank=7):
                dve.wait_ge(ln["var"], n + 1)
                dve.tensor_tensor(inv[0:PN, a, :], ps[0:PN, bank, GN:GN + 2 * GP].rearrange("p (a b) -> p a b", b=2)[:, :, 0],
                                  eps_cols[0:PN, :], ALU.add).then_inc(ln["ve"], 1)

            def normal(dst, n, c, bank=7):
                dve.wait_ge(ln["wide"], n + 1)
                dve.tensor_tensor(dst, c, ps[:, bank, 0:GN], ALU.mult).then_inc(ln["xn"], 1)

            def tokens(g, slot, last=False, first=False):
                for k in range(XT_STEPS):
                    if not last:
                        frames_lo(g + 1, k, 1 - slot)
                    if k == 4 and not first:
                        plus_eps(g - 1)
                    if k == 7 and not first:
                        normal(xn[:, bass.ds((g - 1) * GN, GN)], g - 1, xc)

            for k in range(XT_STEPS):
                frames_lo(0, k, 0)
            dve.wait_ge(s_const, 14)
            dve.tensor_tensor(centring[:, :], ident[:, :], ones_mean[:, :], ALU.subtract).then_inc(s_centring, 1)
            tokens(0, 0, first=True)
            with dve.Fori(0, GROUPS // 2 - 1) as j:
                tokens(2 * j + 1, 1)
                tokens(2 * j + 2, 0)
            tokens(GROUPS - 1, 1, last=True)
            plus_eps(GROUPS - 1)
            normal(xn[:, (GROUPS - 1) * GN:GROUPS * GN], GROUPS - 1, xc)

            dve.wait_ge(s_const, 14)
            dve.wait_ge(ln["xn"], GROUPS)

            def hidden_biases(e, slot):
                dve.tensor_tensor(b1_col[:, 2 * slot:2 * slot + 2, 0], b1T[:, bass.ds(2 * e, 2)], zeros2[:, 0:2],
                                  ALU.add).then_inc(b1_ready, 1)

            dve.wait_ge(s_b1, 1)
            hidden_biases(0, 0)

            def wide_heads(v):
                return v.rearrange("p (h a) -> p h a", a=1).to_broadcast([P, HEADS, N])

            def mask(i, s):
                dve.wait_ge(at_s["q"], i + 1)
                for b in range(2):
                    src = ps[:, s, PN:2 * PN].rearrange("p (n b) -> p b n", b=2)[:, b:b + 1, :]
                    op = dve.tensor_tensor(k_blk[:, s, b, :, :], src.to_broadcast([P, HEADS, N]),
                                           wide_heads(head_mask[:, :]), ALU.mult)
                op.then_inc(at_s["k"], 1)
            def shift(i, s, s4):
                sc = ps[:, 2 + s, 0:HEADS * N].rearrange("p (h n) -> p h n", h=HEADS)
                dve.wait_ge(at_s["s"], i + 1)
                dve.reduce_max(smax[:, s, :], sc, AX_X).then_inc(at_s["mx"], 1)
                dve.wait_ge(at_s["mx"], i + 1)
                dve.tensor_tensor(prob[:, s4, :, :], sc, wide_heads(smax[:, s, :]), ALU.subtract).then_inc(at_s["sub"], 1)

            def total(i, s, first):
                if not first:
                    dve.wait_ge(at_s["p"], i - 1)
                dve.wait_ge(at_s["exp"], i + 1)
                dve.reduce_sum(ssum[:, s % 2, :], prob[:, s, :, :], AX_X).then_inc(at_s["sum"], 1)
                dve.wait_ge(at_s["sum"], i + 1)
                dve.reciprocal(ssum[:, s % 2, :], ssum[:, s % 2, :]).then_inc(at_s["rec"], 1)

            def residual(i):
                dve.wait_ge(at_s["pr"], i + 1)
                own = hT[:, bass.ds(i * PN, PN)]
                dve.scalar_tensor_tensor(out=own, in0=ps[:, 6, 0:PN], scalar=bias_cols[:, 1:2], in1=own,
                                         op0=ALU.add, op1=ALU.add).then_inc(at_s["res"], 1)

            def attend(i, q, t=None):
                if runs(t, 0):
                    mask(i, q % 2)
                if runs(t, 1):
                    shift(i - 1, (q - 1) % 2, (q - 1) % 4)
                if runs(t, 2):
                    total(i - 2, (q - 2) % 4, t in (2, 3))
                if runs(t, 5):
                    residual(i - 5)

            def norm(g, n, q):
                if q == 2:
                    plus_eps(n)
                if q == 3 and not is_last_but_one(g):
                    if not (isinstance(g, int) and g == 0):
                        dve.wait_ge(r_s["xl"], g)
                    normal(xg, n, xc2)

            CHAIN = 2 * ROUNDS + 7

            def wide(v):
                return v.rearrange("p (t a) -> p t a", a=1).to_broadcast([P, RT, E])

            def chain(g, k, op, tick=False):
                op.then_inc(r_s["dve"], 1)
                dve.wait_ge(r_s["dve"], g * CHAIN + k)
                if tick:
                    dve.memset(dve_tick[:, :], 0.0)

            def search(g, rnd, k):
                for t in range(RT):
                    op = dve.max(rtop[:, t, :], rs[:, t, :])
                chain(g, k, op, rnd < ROUNDS - 1)
                if rnd == ROUNDS - 1:
                    k += 1
                    chain(g, k, dve.memset(rtop[:, :, LASTDROP:8], TAKEN), True)
                for t in range(RT):
                    op = dve.match_replace(rs[:, t, :], rtop[:, t, :], rs[:, t, :], TAKEN)
                chain(g, k + 1, op, rnd < ROUNDS - 1)

            def route(g, q, bank=7):
                if q == 0:
                    scores = ps[:, bank, 0:RT * E].rearrange("p (t e) -> p t e", e=E)
                    dve.wait_ge(r_s["lg"], g + 1)
                    chain(g, 1, dve.reduce_max(rmax, scores, AX_X))
                    dve.tensor_tensor(rp, scores, wide(rmax), ALU.subtract).then_inc(r_s["sub"], 1)
                if q == 1:
                    dve.wait_ge(r_s["act"], g + 1)
                    chain(g, 2, dve.reduce_sum(rsum, rp, AX_X))
                    chain(g, 3, dve.reciprocal(rinv, rsum))
                    dve.wait_ge(r_s["neg"], g + 1)
                    dve.tensor_scalar(rneg, rinv, -1.0, None, ALU.mult).then_inc(r_s["inv"], 1)
                    search(g, 0, 4)
                if q == 2:
                    search(g, 1, 6)
                if q == 3:
                    search(g, 2, 8)
                    dve.wait_ge(r_s["ex"], g + 1)
                    chain(g, 11, dve.scalar_tensor_tensor(out=re, in0=rs[:, :, ::-1], scalar=TAKEN / 2 - 0.5, in1=re,
                                                          op0=ALU.is_gt, op1=ALU.mult))
                    chain(g, 12, dve.reduce_sum(rsum, re, AX_X))
                    chain(g, 13, dve.reciprocal(rsum, rsum))
                    dve.tensor_tensor(comb[:, bass.ds(g * GW, GW)].rearrange("p (t e) -> p t e", e=E), re, wide(rsum),
                                      ALU.mult).then_inc(r_s["cw"], 1)

            assert ROUNDS == 3
            turns(dve, attend, norm, route)
            dve.wait_ge(r_s["xl"], GROUPS - 2)
            normal(xg, 2 * GROUPS - 2, xc2)
            route(GROUPS - 2, 0)
            plus_eps(2 * GROUPS - 1, 2, BANK3)
            route(GROUPS - 2, 1)
            route(GROUPS - 2, 2)
            normal(xg3, 2 * GROUPS - 1, xc3, BANK3)
            route(GROUPS - 2, 3)
            for q in range(4):
                route(GROUPS - 1, q, BANK3)

            def mul(m, c, gs, cs, loaded, first):
                s, n = chunks[c]
                if first:
                    dve.wait_ge(c_first[cs][c], 16)
                elif loaded is not None:
                    dve.wait_ge(c_loaded[cs], loaded)
                dve.wait_ge(gelu_done, 2 * m + 2)
                dve.tensor_tensor(gbuf[:, gs, s:s + n], gbuf[:, gs, s:s + n], cbuf[:, cs, s:s + n],
                                  ALU.mult).then_inc(mul_done, 1)

            def low(m, c, gs):
                s, n = chunks[c]
                dve.wait_ge(hi_done, m + 1)
                dve.tensor_tensor(g_lo[:, gs, s:s + n], gbuf[:, gs, s:s + n], g_hi[:, gs, s:s + n].bitcast(F32),
                                  ALU.subtract).then_inc(lo_done, 1)

            def step(n, q, loaded, first, e=None):
                for c in range(NG):
                    if c == 1 and q % 2 == 0 and e is not None:
                        hidden_biases(e + 1, 1 - q // 2)
                    mul(n * NG + c, c, q % 2, q // 2, loaded if c == 0 and q % 2 == 0 else None, loaded is None and q % 2 == 0)
                    if c:
                        low(n * NG + c - 1, c - 1, q % 2)
                    elif not first:
                        low(n * NG - 1, NG - 1, 1 - q % 2)

            for n in range(4):
                step(n, n, None, n == 0, n // 2)
            with dve.Fori(1, HALVES // 4 - 1) as i:
                for q in range(4):
                    step(4 * i + q, q, 16 * i, False, 2 * i + q // 2)
            for q in range(4):
                n = HALVES - 4 + q
                step(n, q, 16 * (n // 4), False, n // 2 if q < 2 else None)
            low(HALVES * NG - 1, NG - 1, 1)

            total = ps[:, 0:NB, :].rearrange("p b n -> p (b n)")
            for g in range(GROUPS):
                cols = slice(g * GN, (g + 1) * GN)
                dve.wait_ge(s_acc, (g + 1) * GN // BLK + 1 if g < GROUPS - 1 else NB)
                dve.tensor_tensor(yT[:, cols].rearrange("p (a b n) -> p a b n", a=GP, b=2),
                                  total[:, cols].rearrange("p (a n b) -> p a b n", a=GP, b=2),
                                  hT[:, cols].rearrange("p (a n b) -> p a b n", a=GP, b=2), ALU.add).then_inc(s_y, 1)


_INS = ["x", "L0_tok_W", "L0_tok_b", "L0_attn_w_qkv", "L0_attn_w_out", "L0_attn_b_out", "L0_ffn_w1", "L0_ffn_b1",
        "L0_ffn_w2", "L0_ffn_b2", "L0_ffn_router_w", "L0_ffn_router_b"]


def kernel(**inputs):
    import numpy as np
    import concourse.bacc as bacc
    from concourse.bass_utils import run_bass_kernel_spmd

    nc = bacc.Bacc("TRN2", target_bir_lowering=False, num_devices=1)
    arrays, args = {}, []
    for name in _INS:
        a = np.ascontiguousarray(inputs[name])
        arrays[f"in_{name}"] = a
        args.append(nc.dram_tensor(f"in_{name}", a.shape, mybir.dt.from_np(a.dtype), kind="ExternalInput").ap())
    clips, frames, width = arrays["in_x"].shape
    patches = -(-(frames - PATCH) // STRIDE) + 1
    y = nc.dram_tensor("out_y", (clips, patches, width), F32, kind="ExternalOutput").ap()
    audio_tower(nc, *args, y)
    r = run_bass_kernel_spmd(nc, [arrays], core_ids=[0])
    return r.results[0]["out_y"]
```
